# Optimizing a Trainium2 kernel written in Bass

```python
import numpy as np
import jax
import jax.numpy as jnp

def _softmax(x, axis=-1):
    return jax.nn.softmax(x, axis=axis)

def _gelu(x):
    return jax.nn.gelu(x, approximate=True)

def _silu(x):
    return jax.nn.silu(x)

def _sigmoid(x):
    return jax.nn.sigmoid(x)

def _layernorm(x, axis=-1, eps=1e-05):
    m = jnp.mean(x, axis=axis, keepdims=True)
    v = jnp.var(x, axis=axis, keepdims=True)
    return (x - m) / jnp.sqrt(v + eps)

def _scatter_add(tgt, idx, src, axis=0):
    return tgt.at[idx].add(src)

def _segment_sum(src, seg, n):
    return jax.ops.segment_sum(src, seg, n)
kernel_name = 'mk_dlrm_tower_d1_rec_r8_eb1186'

def setup_inputs(seed: int=0):
    np.random.seed(seed)
    _w = jnp.asarray

    def _rec_inputs():
        import jax
        import jax.numpy as jnp
        _tk = jax.random.key(seed)
        dense_ctx = jax.random.normal(jax.random.fold_in(_tk, 190), (2048, 16), jnp.float32)
        ids = jnp.stack([jax.random.randint(jax.random.fold_in(_tk, 200 + f), (2048,), 0, v, jnp.int32) for f, v in enumerate([1000, 1000, 12500, 1250, 12500, 125000, 125000, 12500, 12500, 1000, 125000, 1250, 1250, 1000, 1250, 1250, 1000, 1000, 1250, 1000, 1250, 12500, 12500, 1000, 1000, 1250, 1000, 1250, 1000, 12500, 1250, 1250, 1000, 1000, 1250, 1000, 1000, 1250, 1250])], axis=1)
        tbl_0 = 0.05 * jax.random.normal(jax.random.fold_in(_tk, 500 + 0), (1000, 64), jnp.float32)
        tbl_1 = 0.05 * jax.random.normal(jax.random.fold_in(_tk, 500 + 1), (1000, 64), jnp.float32)
        tbl_2 = 0.05 * jax.random.normal(jax.random.fold_in(_tk, 500 + 2), (12500, 64), jnp.float32)
        tbl_3 = 0.05 * jax.random.normal(jax.random.fold_in(_tk, 500 + 3), (1250, 64), jnp.float32)
        tbl_4 = 0.05 * jax.random.normal(jax.random.fold_in(_tk, 500 + 4), (12500, 64), jnp.float32)
        tbl_5 = 0.05 * jax.random.normal(jax.random.fold_in(_tk, 500 + 5), (125000, 64), jnp.float32)
        tbl_6 = 0.05 * jax.random.normal(jax.random.fold_in(_tk, 500 + 6), (125000, 64), jnp.float32)
        tbl_7 = 0.05 * jax.random.normal(jax.random.fold_in(_tk, 500 + 7), (12500, 64), jnp.float32)
        tbl_8 = 0.05 * jax.random.normal(jax.random.fold_in(_tk, 500 + 8), (12500, 64), jnp.float32)
        tbl_9 = 0.05 * jax.random.normal(jax.random.fold_in(_tk, 500 + 9), (1000, 64), jnp.float32)
        tbl_10 = 0.05 * jax.random.normal(jax.random.fold_in(_tk, 500 + 10), (125000, 64), jnp.float32)
        tbl_11 = 0.05 * jax.random.normal(jax.random.fold_in(_tk, 500 + 11), (1250, 64), jnp.float32)
        tbl_12 = 0.05 * jax.random.normal(jax.random.fold_in(_tk, 500 + 12), (1250, 64), jnp.float32)
        tbl_13 = 0.05 * jax.random.normal(jax.random.fold_in(_tk, 500 + 13), (1000, 64), jnp.float32)
        tbl_14 = 0.05 * jax.random.normal(jax.random.fold_in(_tk, 500 + 14), (1250, 64), jnp.float32)
        tbl_15 = 0.05 * jax.random.normal(jax.random.fold_in(_tk, 500 + 15), (1250, 64), jnp.float32)
        tbl_16 = 0.05 * jax.random.normal(jax.random.fold_in(_tk, 500 + 16), (1000, 64), jnp.float32)
        tbl_17 = 0.05 * jax.random.normal(jax.random.fold_in(_tk, 500 + 17), (1000, 64), jnp.float32)
        tbl_18 = 0.05 * jax.random.normal(jax.random.fold_in(_tk, 500 + 18), (1250, 64), jnp.float32)
        tbl_19 = 0.05 * jax.random.normal(jax.random.fold_in(_tk, 500 + 19), (1000, 64), jnp.float32)
        tbl_20 = 0.05 * jax.random.normal(jax.random.fold_in(_tk, 500 + 20), (1250, 64), jnp.float32)
        tbl_21 = 0.05 * jax.random.normal(jax.random.fold_in(_tk, 500 + 21), (12500, 64), jnp.float32)
        tbl_22 = 0.05 * jax.random.normal(jax.random.fold_in(_tk, 500 + 22), (12500, 64), jnp.float32)
        tbl_23 = 0.05 * jax.random.normal(jax.random.fold_in(_tk, 500 + 23), (1000, 64), jnp.float32)
        tbl_24 = 0.05 * jax.random.normal(jax.random.fold_in(_tk, 500 + 24), (1000, 64), jnp.float32)
        tbl_25 = 0.05 * jax.random.normal(jax.random.fold_in(_tk, 500 + 25), (1250, 64), jnp.float32)
        tbl_26 = 0.05 * jax.random.normal(jax.random.fold_in(_tk, 500 + 26), (1000, 64), jnp.float32)
        tbl_27 = 0.05 * jax.random.normal(jax.random.fold_in(_tk, 500 + 27), (1250, 64), jnp.float32)
        tbl_28 = 0.05 * jax.random.normal(jax.random.fold_in(_tk, 500 + 28), (1000, 64), jnp.float32)
        tbl_29 = 0.05 * jax.random.normal(jax.random.fold_in(_tk, 500 + 29), (12500, 64), jnp.float32)
        tbl_30 = 0.05 * jax.random.normal(jax.random.fold_in(_tk, 500 + 30), (1250, 64), jnp.float32)
        tbl_31 = 0.05 * jax.random.normal(jax.random.fold_in(_tk, 500 + 31), (1250, 64), jnp.float32)
        tbl_32 = 0.05 * jax.random.normal(jax.random.fold_in(_tk, 500 + 32), (1000, 64), jnp.float32)
        tbl_33 = 0.05 * jax.random.normal(jax.random.fold_in(_tk, 500 + 33), (1000, 64), jnp.float32)
        tbl_34 = 0.05 * jax.random.normal(jax.random.fold_in(_tk, 500 + 34), (1250, 64), jnp.float32)
        tbl_35 = 0.05 * jax.random.normal(jax.random.fold_in(_tk, 500 + 35), (1000, 64), jnp.float32)
        tbl_36 = 0.05 * jax.random.normal(jax.random.fold_in(_tk, 500 + 36), (1000, 64), jnp.float32)
        tbl_37 = 0.05 * jax.random.normal(jax.random.fold_in(_tk, 500 + 37), (1250, 64), jnp.float32)
        tbl_38 = 0.05 * jax.random.normal(jax.random.fold_in(_tk, 500 + 38), (1250, 64), jnp.float32)
        _rk = jax.random.fold_in(_tk, 7)
        W_top1 = 0.0363456 * jax.random.normal(jax.random.fold_in(_tk, 801), (757, 512), jnp.float32)
        W_top2 = 0.0441942 * jax.random.normal(jax.random.fold_in(_tk, 802), (512, 256), jnp.float32)
        W_top3 = 0.0625 * jax.random.normal(jax.random.fold_in(_tk, 803), (256, 1), jnp.float32)
        b_top1 = jnp.zeros((512,), jnp.float32)
        b_top2 = jnp.zeros((256,), jnp.float32)
        return (dense_ctx, ids, tbl_0, tbl_1, tbl_2, tbl_3, tbl_4, tbl_5, tbl_6, tbl_7, tbl_8, tbl_9, tbl_10, tbl_11, tbl_12, tbl_13, tbl_14, tbl_15, tbl_16, tbl_17, tbl_18, tbl_19, tbl_20, tbl_21, tbl_22, tbl_23, tbl_24, tbl_25, tbl_26, tbl_27, tbl_28, tbl_29, tbl_30, tbl_31, tbl_32, tbl_33, tbl_34, tbl_35, tbl_36, tbl_37, tbl_38, W_top1, b_top1, W_top2, b_top2, W_top3)
    dense_ctx, ids, tbl_0, tbl_1, tbl_2, tbl_3, tbl_4, tbl_5, tbl_6, tbl_7, tbl_8, tbl_9, tbl_10, tbl_11, tbl_12, tbl_13, tbl_14, tbl_15, tbl_16, tbl_17, tbl_18, tbl_19, tbl_20, tbl_21, tbl_22, tbl_23, tbl_24, tbl_25, tbl_26, tbl_27, tbl_28, tbl_29, tbl_30, tbl_31, tbl_32, tbl_33, tbl_34, tbl_35, tbl_36, tbl_37, tbl_38, W_top1, b_top1, W_top2, b_top2, W_top3 = _rec_inputs()

    def _L0_rec_setup():
        import jax, jax.numpy as jnp
        import numpy as np
        NUM_FIELDS = 39
        _ROW, _COL = np.triu_indices(NUM_FIELDS, k=1)
        key = jax.random.key(seed)
        x = jax.random.normal(key, (2048, NUM_FIELDS, 64), dtype=jnp.float32)
        return {'x': x}
    _L0_rec_all = _L0_rec_setup()
    _L0_rec_in = {k: v for k, v in _L0_rec_all.items() if k in ()}
    del _L0_rec_all
    return {'dense_ctx': dense_ctx, 'ids': ids, 'tbl_0': tbl_0, 'tbl_1': tbl_1, 'tbl_2': tbl_2, 'tbl_3': tbl_3, 'tbl_4': tbl_4, 'tbl_5': tbl_5, 'tbl_6': tbl_6, 'tbl_7': tbl_7, 'tbl_8': tbl_8, 'tbl_9': tbl_9, 'tbl_10': tbl_10, 'tbl_11': tbl_11, 'tbl_12': tbl_12, 'tbl_13': tbl_13, 'tbl_14': tbl_14, 'tbl_15': tbl_15, 'tbl_16': tbl_16, 'tbl_17': tbl_17, 'tbl_18': tbl_18, 'tbl_19': tbl_19, 'tbl_20': tbl_20, 'tbl_21': tbl_21, 'tbl_22': tbl_22, 'tbl_23': tbl_23, 'tbl_24': tbl_24, 'tbl_25': tbl_25, 'tbl_26': tbl_26, 'tbl_27': tbl_27, 'tbl_28': tbl_28, 'tbl_29': tbl_29, 'tbl_30': tbl_30, 'tbl_31': tbl_31, 'tbl_32': tbl_32, 'tbl_33': tbl_33, 'tbl_34': tbl_34, 'tbl_35': tbl_35, 'tbl_36': tbl_36, 'tbl_37': tbl_37, 'tbl_38': tbl_38, 'W_top1': W_top1, 'b_top1': b_top1, 'W_top2': W_top2, 'b_top2': b_top2, 'W_top3': W_top3}

def reference(dense_ctx, ids, tbl_0, tbl_1, tbl_2, tbl_3, tbl_4, tbl_5, tbl_6, tbl_7, tbl_8, tbl_9, tbl_10, tbl_11, tbl_12, tbl_13, tbl_14, tbl_15, tbl_16, tbl_17, tbl_18, tbl_19, tbl_20, tbl_21, tbl_22, tbl_23, tbl_24, tbl_25, tbl_26, tbl_27, tbl_28, tbl_29, tbl_30, tbl_31, tbl_32, tbl_33, tbl_34, tbl_35, tbl_36, tbl_37, tbl_38, W_top1, b_top1, W_top2, b_top2, W_top3):
    import jax
    import jax.numpy as jnp

    def _L0_rec_ref(x):
        import jax, jax.numpy as jnp
        import numpy as np
        NUM_FIELDS = 39
        _ROW, _COL = np.triu_indices(NUM_FIELDS, k=1)
        s = jnp.sum(x, axis=-1)
        return s[:, _ROW] * s[:, _COL]
    e = jnp.stack([tbl_0[ids[:, 0]], tbl_1[ids[:, 1]], tbl_2[ids[:, 2]], tbl_3[ids[:, 3]], tbl_4[ids[:, 4]], tbl_5[ids[:, 5]], tbl_6[ids[:, 6]], tbl_7[ids[:, 7]], tbl_8[ids[:, 8]], tbl_9[ids[:, 9]], tbl_10[ids[:, 10]], tbl_11[ids[:, 11]], tbl_12[ids[:, 12]], tbl_13[ids[:, 13]], tbl_14[ids[:, 14]], tbl_15[ids[:, 15]], tbl_16[ids[:, 16]], tbl_17[ids[:, 17]], tbl_18[ids[:, 18]], tbl_19[ids[:, 19]], tbl_20[ids[:, 20]], tbl_21[ids[:, 21]], tbl_22[ids[:, 22]], tbl_23[ids[:, 23]], tbl_24[ids[:, 24]], tbl_25[ids[:, 25]], tbl_26[ids[:, 26]], tbl_27[ids[:, 27]], tbl_28[ids[:, 28]], tbl_29[ids[:, 29]], tbl_30[ids[:, 30]], tbl_31[ids[:, 31]], tbl_32[ids[:, 32]], tbl_33[ids[:, 33]], tbl_34[ids[:, 34]], tbl_35[ids[:, 35]], tbl_36[ids[:, 36]], tbl_37[ids[:, 37]], tbl_38[ids[:, 38]]], axis=1)
    z = _L0_rec_ref(e)
    z = z.reshape(z.shape[0], -1)
    h = jnp.concatenate([z, dense_ctx], axis=1)
    h = jnp.maximum(h @ W_top1 + b_top1, 0.0)
    h = jnp.maximum(h @ W_top2 + b_top2, 0.0)
    y = h @ W_top3
    return y

_drawn_inputs = setup_inputs


def setup_inputs(seed=0):
    import zlib

    import numpy as np

    out = dict(_drawn_inputs(seed))
    spreads = {'b_top1': (0.0, 0.1), 'b_top2': (0.0, 0.1)}
    factors = {}
    for name, (base, spread) in spreads.items():
        noise = np.random.default_rng([zlib.crc32(name.encode()), seed]).standard_normal(out[name].shape)
        drawn = base * np.exp(spread * noise) if base else spread * noise
        out[name] = jnp.asarray(drawn.astype(out[name].dtype))
    for name, factor in factors.items():
        out[name] = (out[name] * factor).astype(out[name].dtype)
    return out
```

```python
import numpy as np
import concourse.bass as bass
from concourse import mybir
from contextlib import ExitStack

P = 128
B = 2048
T = B // P
NF = 39
D = 64
ND = NF // 2
NPAIR = NF * ND
NDENSE = 16
K1 = 6
COLS = K1 * P
N1 = 512
N2 = 256
M1 = N1 // P
M2 = N2 // P
TT = 2
NB = TT * P
STEPS = T // TT


def build(nc, ids, dense, tables, w1, w2, b2, w3, out):
    f32 = mybir.dt.float32
    f32r = mybir.dt.float32r
    i32 = mybir.dt.int32
    ALU = mybir.AluOpType
    ACT = mybir.ActivationFunctionType
    AX = mybir.AxisListType
    NG = len(tables)

    with ExitStack() as ctx:
        def sb(name, shape, dt=f32):
            return ctx.enter_context(nc.sbuf_tensor(name, shape, dt))

        def sem(name):
            return ctx.enter_context(nc.semaphore(name))

        ids_sb = sb("ids_sb", [P, T * NF], i32)
        index = sb("index", [P, 2, TT * NG], i32)
        rows = sb("rows", [P, 2, TT * NG * D])
        s = sb("s", [P, T, NF + ND])
        z = sb("z", [P, 2, TT, COLS])
        dense_sb = sb("dense_sb", [P, T, NDENSE])
        ident = sb("ident", [P, P])
        w1_raw = sb("w1_raw", [P, K1, N1])
        w2_raw = sb("w2_raw", [P, M1, N2])
        w1_hi, w1_lo = sb("w1_hi", [P, K1, N1], f32r), sb("w1_lo", [P, K1, N1], f32r)
        w2_hi, w2_lo = sb("w2_hi", [P, M1, N2], f32r), sb("w2_lo", [P, M1, N2], f32r)
        b2_sb = sb("b2_sb", [P, M2])
        w3_sb = sb("w3_sb", [P, M2])
        zt_hi, zt_lo = sb("zt_hi", [P, K1, NB], f32r), sb("zt_lo", [P, K1, NB], f32r)
        h1_hi, h1_lo = sb("h1_hi", [P, M1, NB], f32r), sb("h1_lo", [P, M1, NB], f32r)
        h2 = sb("h2", [P, M2, NB])
        y = sb("y", [P, T])

        zt_ps = [ctx.enter_context(nc.psum_tensor(f"zt_ps{b}", [P, 2 * NB], f32)) for b in range(2)]
        h1_ps = [ctx.enter_context(nc.psum_tensor(f"h1_ps{b}", [P, 2 * NB], f32)) for b in range(2)]
        h2_ps = ctx.enter_context(nc.psum_tensor("h2_ps", [P, M2 * NB], f32))

        ids_in, dense_in, w1_in, w2_in = sem("ids_in"), sem("dense_in"), sem("w1_in"), sem("w2_in")
        small_in, y_out = sem("small_in"), sem("y_out")
        gathered = [sem("gathered0"), sem("gathered1")]
        ident_zero, ident_made, pad_made = sem("ident_zero"), sem("ident_made"), sem("pad_made")
        index_made, dense_copied = sem("index_made"), sem("dense_copied")
        s_made, s_doubled, z_made = sem("s_made"), sem("s_doubled"), sem("z_made")
        w1_hi_made, w2_hi_made, w1_split, w2_split = (sem("w1_hi_made"), sem("w2_hi_made"),
                                                      sem("w1_split"), sem("w2_split"))
        zt_done, zt_hi_made, zt_lo_made = sem("zt_done"), sem("zt_hi_made"), sem("zt_lo_made")
        h1_done, h1_hi_made, h1_lo_made = sem("h1_done"), sem("h1_hi_made"), sem("h1_lo_made")
        h2_done, h2_made, y_done, y_made = sem("h2_done"), sem("h2_made"), sem("y_done"), sem("y_made")

        block = ctx.enter_context(nc.Block())

        @block.sync
        def _(sp):
            sp.dma_start(ids_sb[:, :], ids.rearrange("(p t) f -> p (t f)", t=T)).then_inc(ids_in, 16)
            sp.dma_start(w1_raw[:, :, :], w1.rearrange("(k p) n -> p k n", p=P)).then_inc(w1_in, 16)
            sp.dma_start(dense_sb[:, :, :], dense.rearrange("(p t) d -> p t d", t=T)).then_inc(dense_in, 16)
            sp.dma_start(w2_raw[:, :, :], w2.rearrange("(k p) n -> p k n", p=P)).then_inc(w2_in, 16)
            sp.dma_start(b2_sb[:, :], b2).then_inc(small_in, 16)
            sp.dma_start(w3_sb[:, :], w3).then_inc(small_in, 16)
            sp.wait_ge(y_made, STEPS)
            sp.dma_start(out.rearrange("(p t) o -> p (t o)", t=T), y[:, :]).then_inc(y_out, 16)
            sp.wait_ge(y_out, 16)

        @block.gpsimd
        def _(pool):
            def gather(g, slot):
                nc.gpsimd.tensor_copy(index[:, slot, :],
                                      ids_sb[:, bass.ds(g * (TT * NF), TT * NF)]).then_inc(index_made, 1)
                pool.wait_ge(index_made, g + 1)
                pool.nop(nofuse=True)
                for q in range(TT * NG):
                    nc.gpsimd.indirect_dma_start(
                        out=rows[:, slot, q * D:(q + 1) * D], out_offset=None, in_=tables[q % NG],
                        in_offset=bass.IndirectOffsetOnAxis(ap=index[:, slot, q:q + 1], axis=0),
                    ).then_inc(gathered[slot], 16)

            nc.gpsimd.memset(ident[:, :], 0.0).then_inc(ident_zero, 1)
            pool.wait_ge(ident_zero, 1)
            nc.gpsimd.affine_select(out=ident[:, :], in_=ident[:, :], compare_op=ALU.not_equal, fill=1.0,
                                    base=0, pattern=[[-1, P]], channel_multiplier=1).then_inc(ident_made, 1)
            nc.gpsimd.memset(z[:, :, :, NPAIR + NDENSE:NPAIR + NDENSE + 1], 1.0).then_inc(pad_made, 1)
            nc.gpsimd.memset(z[:, :, :, NPAIR + NDENSE + 1:COLS], 0.0).then_inc(pad_made, 1)
            pool.wait_ge(ids_in, 16)
            gather(0, 0)
            gather(1, 1)
            with pool.Fori(0, (STEPS - 2) // 2) as i:
                for slot in range(2):
                    g = 2 * i + 2 + slot
                    pool.wait_ge(s_made, g - 1)
                    gather(g, slot)

        @block.vector
        def _(dve):
            def pairs(g, slot, uses):
                now = bass.ds(g * TT, TT)
                dve.wait_ge(gathered[slot], TT * NG * 16 * uses)
                nc.vector.tensor_reduce(s[:, now, 0:NF],
                                        rows[:, slot, :].rearrange("p (t f d) -> p t f d", t=TT, d=D),
                                        axis=AX.X, op=ALU.add).then_inc(s_made, 1)
                dve.wait_ge(s_made, g + 1)
                nc.vector.tensor_copy(s[:, now, NF:NF + ND], s[:, now, 0:ND]).then_inc(s_doubled, 1)
                nc.vector.tensor_copy(z[:, slot, :, NPAIR:NPAIR + NDENSE],
                                      dense_sb[:, now, :]).then_inc(dense_copied, 1)
                dve.wait_ge(s_doubled, g + 1)
                window = bass.AP(s, 1, [[T * (NF + ND), P], [NF + ND, T], [1, ND], [1, NF]])
                nc.vector.tensor_tensor(
                    z[:, slot, :, 0:NPAIR].rearrange("p t (d i) -> p t d i", d=ND),
                    s[:, now, 0:NF].unsqueeze(2).broadcast_to((P, TT, ND, NF)),
                    window[:, now], ALU.mult).then_inc(z_made, 1)

            def zt_low(g, parity):
                for c in range(3):
                    dve.wait_ge(zt_hi_made, 3 * g + c + 1)
                    nc.vector.tensor_tensor(
                        zt_lo[:, 2 * c:2 * c + 2, :].rearrange("p k b -> p (k b)"),
                        zt_ps[(3 * parity + c) % 2][:, :],
                        zt_hi[:, 2 * c:2 * c + 2, :].rearrange("p k b -> p (k b)").bitcast(f32),
                        ALU.subtract).then_inc(zt_lo_made, 1)

            def h1_low(g):
                for c in range(2):
                    dve.wait_ge(h1_hi_made, 2 * g + c + 1)
                    nc.vector.scalar_tensor_tensor(
                        out=h1_lo[:, 2 * c:2 * c + 2, :].rearrange("p k b -> p (k b)"),
                        in0=h1_ps[c][:, :], scalar=0.0,
                        in1=h1_hi[:, 2 * c:2 * c + 2, :].rearrange("p k b -> p (k b)").bitcast(f32),
                        op0=ALU.max, op1=ALU.subtract).then_inc(h1_lo_made, 1)

            dve.wait_ge(dense_in, 16)
            dve.wait_ge(w1_hi_made, 1)
            nc.vector.tensor_tensor(w1_lo[:, :, :], w1_raw[:, :, :], w1_hi[:, :, :].bitcast(f32),
                                    ALU.subtract).then_inc(w1_split, 1)
            dve.wait_ge(w2_hi_made, 1)
            nc.vector.tensor_tensor(w2_lo[:, :, :], w2_raw[:, :, :], w2_hi[:, :, :].bitcast(f32),
                                    ALU.subtract).then_inc(w2_split, 1)
            pairs(0, 0, 1)
            zt_low(0, 0)
            pairs(1, 1, 1)
            h1_low(0)
            zt_low(1, 1)
            pairs(2, 0, 2)
            with dve.Fori(0, (STEPS - 4) // 2) as i:
                for j in range(2):
                    g = 2 * i + 1 + j
                    h1_low(g)
                    zt_low(g + 1, j)
                    pairs(g + 2, 1 - j, i + 2 + j)
            for g in range(STEPS - 3, STEPS):
                h1_low(g)
                if g + 1 < STEPS:
                    zt_low(g + 1, (g + 1) % 2)
                if g + 2 < STEPS:
                    pairs(g + 2, g % 2, (g + 2) // 2 + 1)

        @block.scalar
        def _(act):
            def zt_high(g, parity):
                for c in range(3):
                    act.wait_ge(zt_done, 3 * g + c + 1)
                    nc.scalar.activation(zt_hi[:, 2 * c:2 * c + 2, :].rearrange("p k b -> p (k b)"),
                                         zt_ps[(3 * parity + c) % 2][:, :], ACT.Copy).then_inc(zt_hi_made, 1)

            def layers(g, parity, last=False):
                for c in range(2):
                    act.wait_ge(h1_done, 2 * g + c + 1)
                    nc.scalar.activation(h1_hi[:, 2 * c:2 * c + 2, :].rearrange("p k b -> p (k b)"),
                                         h1_ps[c][:, :], ACT.Relu).then_inc(h1_hi_made, 1)
                if not last:
                    zt_high(g + 1, 1 - parity)
                act.wait_ge(h2_done, g + 1)
                for m in range(M2):
                    nc.scalar.activation(h2[:, m, :], h2_ps[:, m * NB:(m + 1) * NB], ACT.Relu,
                                         bias=b2_sb[:, m:m + 1]).then_inc(h2_made, 1)
                act.wait_ge(y_done, g + 1)
                nc.scalar.activation(y[:, bass.ds(g * TT, TT)], h2_ps[:, 0:TT], ACT.Copy).then_inc(y_made, 1)

            act.wait_ge(w1_in, 16)
            nc.scalar.activation(w1_hi[:, :, :], w1_raw[:, :, :], ACT.Copy).then_inc(w1_hi_made, 1)
            act.wait_ge(w2_in, 16)
            nc.scalar.activation(w2_hi[:, :, :], w2_raw[:, :, :], ACT.Copy).then_inc(w2_hi_made, 1)
            act.wait_ge(small_in, 32)
            zt_high(0, 0)
            layers(0, 0)
            with act.Fori(0, (STEPS - 2) // 2) as i:
                for j in range(2):
                    layers(2 * i + 1 + j, 1 - j)
            layers(STEPS - 1, 1, last=True)

        @block.tensor
        def _(pe):
            def transpose_z(g, parity, first=False):
                for c in range(3):
                    if not (first and c < 2):
                        pe.wait_ge(zt_lo_made, 3 * g + c - 1)
                    for k in range(2):
                        for t in range(TT):
                            last = nc.tensor.transpose(
                                zt_ps[(3 * parity + c) % 2][:, (k * TT + t) * P:(k * TT + t + 1) * P],
                                z[:, parity, t, (2 * c + k) * P:(2 * c + k + 1) * P], ident[:, :])
                    last.then_inc(zt_done, 1)

            def product(out_ap, lhs, rhs, n_chunks, m):
                terms = [(0, 0), (0, 1), (1, 0)]
                for k in range(n_chunks):
                    for a, b in terms:
                        last = nc.tensor.matmul(out_ap, lhs[a][:, k, m * P:(m + 1) * P], rhs[b][:, k, :],
                                                start=(k == 0 and (a, b) == terms[0]),
                                                stop=(k == n_chunks - 1 and (a, b) == terms[-1]))
                return last

            def step(g, parity, first=False, last_step=False):
                pe.wait_ge(zt_lo_made, 3 * (g + 1))
                for m in range(M1):
                    last = product(h1_ps[m // 2][:, (m % 2) * NB:(m % 2 + 1) * NB], (w1_hi, w1_lo),
                                   (zt_hi, zt_lo), K1, m)
                    if m % 2:
                        last.then_inc(h1_done, 1)
                if not last_step:
                    pe.wait_ge(z_made, g + 2)
                    pe.wait_ge(dense_copied, g + 2)
                    transpose_z(g + 1, 1 - parity)
                if not first:
                    pe.wait_ge(y_made, g)
                pe.wait_ge(h1_lo_made, 2 * (g + 1))
                for m in range(M2):
                    last = product(h2_ps[:, m * NB:(m + 1) * NB], (w2_hi, w2_lo), (h1_hi, h1_lo), M1, m)
                last.then_inc(h2_done, 1)
                pe.wait_ge(h2_made, M2 * (g + 1))
                for t in range(TT):
                    for m in range(M2):
                        last = nc.tensor.matmul(h2_ps[:, t:t + 1], h2[:, m, t * P:(t + 1) * P],
                                                w3_sb[:, m:m + 1], start=(m == 0), stop=(m == M2 - 1))
                last.then_inc(y_done, 1)

            pe.wait_ge(ident_made, 1)
            pe.wait_ge(pad_made, 2)
            pe.wait_ge(z_made, 1)
            pe.wait_ge(dense_copied, 1)
            transpose_z(0, 0, first=True)
            pe.wait_ge(w1_split, 1)
            pe.wait_ge(w2_split, 1)
            step(0, 0, first=True)
            with pe.Fori(0, (STEPS - 2) // 2) as i:
                for j in range(2):
                    step(2 * i + 1 + j, 1 - j)
            step(STEPS - 1, 1, last_step=True)


def pair_rows():
    number = {}
    for i in range(NF):
        for j in range(i + 1, NF):
            number[i, j] = len(number)
    return [number[min(i, (i + d) % NF), max(i, (i + d) % NF)] for d in range(1, ND + 1) for i in range(NF)]


def kernel(**inputs):
    import concourse.bacc as bacc
    from concourse.bass_utils import run_bass_kernel_spmd as run

    nc = bacc.Bacc("TRN2", target_bir_lowering=False, num_devices=1)
    arrays = {}

    def put(name, a):
        a = np.ascontiguousarray(a)
        arrays[f"in_{name}"] = a
        return nc.dram_tensor(f"in_{name}", a.shape, mybir.dt.from_np(a.dtype), kind="ExternalInput").ap()

    w1 = np.asarray(inputs["W_top1"])
    laid = np.zeros((COLS, N1), w1.dtype)
    laid[:NPAIR] = w1[pair_rows()]
    laid[NPAIR:NPAIR + NDENSE] = w1[NPAIR:]
    laid[NPAIR + NDENSE] = np.asarray(inputs["b_top1"])
    args = [put("ids", inputs["ids"]), put("dense_ctx", inputs["dense_ctx"]),
            [put(f"tbl_{f}", inputs[f"tbl_{f}"]) for f in range(NF)],
            put("w1", laid), put("w2", inputs["W_top2"]),
            put("b2", np.asarray(inputs["b_top2"]).reshape(M2, P).T),
            put("w3", np.asarray(inputs["W_top3"]).reshape(M2, P).T)]
    out = nc.dram_tensor("out_0", (B, 1), mybir.dt.float32, kind="ExternalOutput").ap()
    build(nc, *args, out)
    r = run(nc, [arrays], core_ids=[0])
    return r.results[0]["out_0"]
```

```python
import numpy as np
import concourse.bass as bass
from concourse import mybir
from contextlib import ExitStack

P = 128
B = 2048
T = B // P
VOCAB = [1000, 1000, 12500, 1250, 12500, 125000, 125000, 12500, 12500, 1000, 125000, 1250, 1250,
         1000, 1250, 1250, 1000, 1000, 1250, 1000, 1250, 12500, 12500, 1000, 1000, 1250, 1000, 1250,
         1000, 12500, 1250, 1250, 1000, 1000, 1250, 1000, 1000, 1250, 1250]
NF = len(VOCAB)
D = 64
ND = NF // 2
NPAIR = NF * ND
NDENSE = 16
K1 = 6
COLS = K1 * P
N1 = 512
N2 = 256
M1 = N1 // P
M2 = N2 // P
TT = 2
NB = TT * P
STEPS = T // TT

N_BIG = 1
AHEAD = 4
ROWS_PER_PIECE = 32
PIECE_SLOTS = 4
A_RING = 4
SEL_RING = 2

SMALL_LOW = 32
BIG_LOW = P
BIG_COLS = -(-12500 // BIG_LOW)


def plan():
    big = [f for f in range(NF) if VOCAB[f] > 1250]
    big.sort(key=lambda f: VOCAB[f])
    streamed, gathered = big[:N_BIG], big[N_BIG:]
    left = sorted((f for f in range(NF) if VOCAB[f] <= 1250), key=lambda f: -VOCAB[f])
    groups = []
    while left:
        group, used = [], 0
        for f in list(left):
            need = -(-VOCAB[f] // SMALL_LOW)
            if len(group) < P // SMALL_LOW and used + need <= P:
                group.append((f, used))
                used += need
                left.remove(f)
        groups.append(group)
    return gathered, streamed, groups


GATHERED, STREAMED, GROUPS = plan()
NG = len(GATHERED)
NS = len(GROUPS)
NQ = NS + N_BIG
ORDER = GATHERED + STREAMED + [f for group in GROUPS for f, _ in group]
F = NF - NG
KF = 4 * F + 1
S_STRIDE = F + 4
FIRST = [N_BIG + sum(len(g) for g in GROUPS[:q]) for q in range(NS)]
BIG_PIECES = [min(ROWS_PER_PIECE, BIG_COLS - c) for c in range(0, BIG_COLS, ROWS_PER_PIECE)]
CENTRE = (P // 2, BIG_COLS // 2)


def build(nc, ids, dense, tables, small_rows, big_rows, coef, const, w1, w2, b2, w3, out):
    f32 = mybir.dt.float32
    f32r = mybir.dt.float32r
    i32 = mybir.dt.int32
    ALU = mybir.AluOpType
    ACT = mybir.ActivationFunctionType
    AX = mybir.AxisListType

    with ExitStack() as ctx:
        def sb(name, shape, dt=f32):
            return ctx.enter_context(nc.sbuf_tensor(name, shape, dt))

        def bank(name):
            return ctx.enter_context(nc.psum_tensor(name, [P, 2 * NB], f32))

        def sem(name):
            return ctx.enter_context(nc.semaphore(name))

        ids_sb = sb("ids_sb", [P, T, NF], i32)
        index = sb("index", [P, 2, TT, NG], i32)
        rows = sb("rows", [P, 2, TT, NG * D])
        digits = sb("digits", [P, T, 2 * F], i32)
        feat = sb("feat", [P, T, KF])
        featT = sb("featT", [P, T * P], f32r)
        coef_raw = sb("coef_raw", [P, NQ * 2 * P])
        coef_sb = sb("coef_sb", [P, NQ, 2, P], f32r)
        NC = const.shape[1]
        const_sb = sb("const_sb", [P, NC])
        blocks = const_sb[:, 0:4 * NS].rearrange("p (q j) -> p q j", j=4)
        ones4 = const_sb[:, 4 * NS:4 * NS + 4]
        ones1 = const_sb[:, 4 * NS + 4:4 * NS + 5]
        centre = const_sb[:, 4 * NS + 5:NC]
        piece = sb("piece", [P, PIECE_SLOTS, ROWS_PER_PIECE * D])
        sums = sb("sums", [P, NS, SMALL_LOW])
        table = sb("table", [P, NQ, P])
        table_hi, table_lo = sb("table_hi", [P, NQ, P], f32r), sb("table_lo", [P, NQ, P], f32r)
        onehot = sb("onehot", [P, A_RING, 2, NB], f32r)
        kept = sb("kept", [P, SEL_RING, NB])
        s = sb("s", [P, T, NF + ND])
        z = sb("z", [P, 2, TT, COLS])
        dense_sb = sb("dense_sb", [P, T, NDENSE])
        ident = sb("ident", [P, P])
        w1_raw = sb("w1_raw", [P, K1, N1])
        w2_raw = sb("w2_raw", [P, M1, N2])
        w1_hi, w1_lo = sb("w1_hi", [P, K1, N1], f32r), sb("w1_lo", [P, K1, N1], f32r)
        w2_hi, w2_lo = sb("w2_hi", [P, M1, N2], f32r), sb("w2_lo", [P, M1, N2], f32r)
        b2_sb = sb("b2_sb", [P, M2])
        w3_sb = sb("w3_sb", [P, M2])
        zt_hi, zt_lo = sb("zt_hi", [P, K1 * NB], f32r), sb("zt_lo", [P, K1 * NB], f32r)
        h1_hi, h1_lo = sb("h1_hi", [P, M1 * NB], f32r), sb("h1_lo", [P, M1 * NB], f32r)
        h2 = sb("h2", [P, M2, NB])
        y = sb("y", [P, T])

        zt_ps = [bank("zt_ps0"), bank("zt_ps1")]
        h1_ps = [bank("h1_ps0"), bank("h1_ps1")]
        h2_ps = bank("h2_ps")
        a_ps = bank("a_ps")
        sel_ps = bank("sel_ps")
        s_ps = bank("s_ps")
        a_banks = [a_ps, zt_ps[0], zt_ps[1], h2_ps]
        sel_banks = [sel_ps, h1_ps[0]]
        s_view = s_ps[:, 0:AHEAD * TT * S_STRIDE].rearrange("p (t c) -> p t c", c=S_STRIDE)

        ids_in, const_in, coef_in = sem("ids_in"), sem("const_in"), sem("coef_in")
        piece_in = [sem(f"piece_in{n}") for n in range(PIECE_SLOTS)]
        dense_in, w1_in, w2_in, small_in, y_out = (sem("dense_in"), sem("w1_in"), sem("w2_in"),
                                                   sem("small_in"), sem("y_out"))
        gathered = [sem("gathered0"), sem("gathered1")]
        ident_zero, ident_made, pad_made, index_made = (sem("ident_zero"), sem("ident_made"),
                                                        sem("pad_made"), sem("index_made"))
        digits_made, feat_made, featT_done, featT_made = (sem("digits_made"), sem("feat_made"),
                                                          sem("featT_done"), sem("featT_made"))
        coef_made, table_zero, piece_summed = sem("coef_made"), sem("table_zero"), sem("piece_summed")
        table_made, table_hi_made, table_split = (sem("table_made"), sem("table_hi_made"),
                                                  sem("table_split"))
        a_done, onehot_made, sel_done, kept_made = (sem("a_done"), sem("onehot_made"), sem("sel_done"),
                                                    sem("kept_made"))
        looked_done, looked_made = sem("looked_done"), sem("looked_made")
        summed, s_doubled, z_made, dense_copied = (sem("summed"), sem("s_doubled"), sem("z_made"),
                                                   sem("dense_copied"))
        w1_hi_made, w2_hi_made, w1_split, w2_split = (sem("w1_hi_made"), sem("w2_hi_made"),
                                                      sem("w1_split"), sem("w2_split"))
        zt_done, zt_hi_made, zt_lo_made = sem("zt_done"), sem("zt_hi_made"), sem("zt_lo_made")
        h1_done, h1_hi_made, h1_lo_made = sem("h1_done"), sem("h1_hi_made"), sem("h1_lo_made")
        h2_done, h2_made, y_done, y_made = sem("h2_done"), sem("h2_made"), sem("y_done"), sem("y_made")

        pieces = [(q, 0, SMALL_LOW) for q in range(NS)]
        for x in range(N_BIG):
            pieces += [(NS + x, ROWS_PER_PIECE * c, n) for c, n in enumerate(BIG_PIECES)]
        LOOKING = STEPS - AHEAD

        block = ctx.enter_context(nc.Block())

        @block.sync
        def _(sp):
            sp.dma_start(ids_sb[:, :, :], ids.rearrange("(p t) f -> p t f", t=T)).then_inc(ids_in, 16)
            sp.dma_start(const_sb[:, :], const).then_inc(const_in, 16)
            sp.dma_start(coef_raw[0:KF, :], coef).then_inc(coef_in, 16)
            for n, (q, col, count) in enumerate(pieces):
                if n >= PIECE_SLOTS:
                    sp.wait_ge(piece_summed, n - PIECE_SLOTS + 1)
                src = (small_rows[q] if q < NS
                       else big_rows[q - NS][:, col * D:(col + count) * D])
                sp.dma_start(piece[:, n % PIECE_SLOTS, 0:count * D], src).then_inc(
                    piece_in[n % PIECE_SLOTS], 16)
                if n == PIECE_SLOTS:
                    sp.dma_start(w1_raw[:, :, :], w1.rearrange("(k p) n -> p k n", p=P)).then_inc(w1_in, 16)
                    sp.dma_start(w2_raw[:, :, :], w2.rearrange("(k p) n -> p k n", p=P)).then_inc(w2_in, 16)
                    sp.dma_start(dense_sb[:, :, :],
                                 dense.rearrange("(p t) d -> p t d", t=T)).then_inc(dense_in, 16)
                    sp.dma_start(b2_sb[:, :], b2).then_inc(small_in, 16)
                    sp.dma_start(w3_sb[:, :], w3).then_inc(small_in, 16)
            sp.wait_ge(y_made, STEPS)
            sp.dma_start(out.rearrange("(p t) o -> p (t o)", t=T), y[:, :]).then_inc(y_out, 16)
            sp.wait_ge(y_out, 16)

        @block.gpsimd
        def _(pool):
            def gather(g, slot):
                nc.gpsimd.tensor_copy(index[:, slot, :, :],
                                      ids_sb[:, bass.ds(g * TT, TT), 0:NG]).then_inc(index_made, 1)
                pool.wait_ge(index_made, g + 1)
                pool.nop(nofuse=True)
                for t in range(TT):
                    for f in range(NG):
                        nc.gpsimd.indirect_dma_start(
                            out=rows[:, slot, t, f * D:(f + 1) * D], out_offset=None, in_=tables[f],
                            in_offset=bass.IndirectOffsetOnAxis(ap=index[:, slot, t, f:f + 1], axis=0),
                        ).then_inc(gathered[slot], 16)

            nc.gpsimd.memset(ident[:, :], 0.0).then_inc(ident_zero, 1)
            pool.wait_ge(ident_zero, 1)
            nc.gpsimd.affine_select(out=ident[:, :], in_=ident[:, :], compare_op=ALU.not_equal, fill=1.0,
                                    base=0, pattern=[[-1, P]], channel_multiplier=1).then_inc(ident_made, 1)
            nc.gpsimd.memset(z[:, :, :, NPAIR + NDENSE:NPAIR + NDENSE + 1], 1.0).then_inc(pad_made, 1)
            nc.gpsimd.memset(z[:, :, :, NPAIR + NDENSE + 1:COLS], 0.0).then_inc(pad_made, 1)
            pool.wait_ge(ids_in, 16)
            gather(0, 0)
            gather(1, 1)
            with pool.Fori(0, (STEPS - 2) // 2) as i:
                for slot in range(2):
                    g = 2 * i + 2 + slot
                    pool.wait_ge(summed, TT * (g - 1))
                    gather(g, slot)

        @block.vector
        def _(dve):
            def features():
                nc.vector.memset(feat[:, :, 4 * F:KF], 1.0).then_inc(feat_made, 1)
                nc.vector.memset(table[:, NS:NQ, BIG_COLS:P], 0.0).then_inc(table_zero, 1)
                dve.wait_ge(ids_in, 16)
                big, small = ids_sb[:, :, NG:NG + N_BIG], ids_sb[:, :, NG + N_BIG:NF]
                nc.vector.tensor_scalar(digits[:, :, 0:N_BIG], big, BIG_LOW - 1, None,
                                        ALU.bitwise_and).then_inc(digits_made, 1)
                nc.vector.tensor_scalar(digits[:, :, F:F + N_BIG], big, 7, None,
                                        ALU.logical_shift_right).then_inc(digits_made, 1)
                nc.vector.tensor_scalar(digits[:, :, N_BIG:F], small, 5, None,
                                        ALU.logical_shift_right).then_inc(digits_made, 1)
                nc.vector.tensor_scalar(digits[:, :, F + N_BIG:2 * F], small, SMALL_LOW - 1, None,
                                        ALU.bitwise_and).then_inc(digits_made, 1)
                dve.wait_ge(const_in, 16)
                dve.wait_ge(digits_made, 4)
                nc.vector.tensor_tensor(feat[:, :, 0:2 * F], digits[:, :, :],
                                        centre.unsqueeze(1).broadcast_to((P, T, 2 * F)),
                                        ALU.subtract).then_inc(feat_made, 1)
                dve.wait_ge(feat_made, 2)
                nc.vector.tensor_tensor(feat[:, :, 2 * F:4 * F], feat[:, :, 0:2 * F], feat[:, :, 0:2 * F],
                                        ALU.mult).then_inc(feat_made, 1)

            def make_table(q):
                for n, (of, col, count) in enumerate(pieces):
                    if of == q:
                        dve.wait_ge(piece_in[n % PIECE_SLOTS], 16 * (n // PIECE_SLOTS + 1))
                        to = sums[:, q, :] if q < NS else table[:, q, col:col + count]
                        nc.vector.tensor_reduce(
                            to, piece[:, n % PIECE_SLOTS, 0:count * D].rearrange("p (r d) -> p r d", d=D),
                            axis=AX.X, op=ALU.add).then_inc(piece_summed, 1)
                        last_piece = n
                dve.wait_ge(piece_summed, last_piece + 1)
                if q < NS:
                    nc.vector.tensor_tensor(
                        table[:, q, :].rearrange("p (j c) -> p j c", j=4),
                        sums[:, q, :].unsqueeze(1).broadcast_to((P, 4, SMALL_LOW)),
                        blocks[:, q, :].unsqueeze(2).broadcast_to((P, 4, SMALL_LOW)),
                        ALU.mult).then_inc(table_made, 1)
                    dve.wait_ge(table_made, q + 1)
                else:
                    dve.wait_ge(table_zero, 1)
                nc.vector.tensor_copy(table_hi[:, q, :], table[:, q, :]).then_inc(table_hi_made, 1)
                dve.wait_ge(table_hi_made, q + 1)
                nc.vector.tensor_tensor(table_lo[:, q, :], table[:, q, :], table_hi[:, q, :].bitcast(f32),
                                        ALU.subtract).then_inc(table_split, 1)

            def keep(n, a_slot, sel_bank, slot):
                dve.wait_ge(sel_done, n + 1)
                nc.vector.tensor_tensor(kept[:, slot, :], onehot[:, a_slot, 1, :].bitcast(f32),
                                        sel_bank[:, 0:NB], ALU.mult).then_inc(kept_made, 1)

            def row_sums(g, slot, t, uses):
                dve.wait_ge(gathered[slot], TT * NG * 16 * uses)
                nc.vector.tensor_reduce(s[:, bass.ds(g * TT + t, 1), 0:NG],
                                        rows[:, slot, t, :].rearrange("p (o f d) -> p o f d", o=1, d=D),
                                        axis=AX.X, op=ALU.add).then_inc(summed, 1)

            def double(g):
                dve.wait_ge(summed, TT * (g + 1))
                dve.wait_ge(looked_made, g + 1)
                nc.vector.tensor_copy(s[:, bass.ds(g * TT, TT), NF:NF + ND],
                                      s[:, bass.ds(g * TT, TT), 0:ND]).then_inc(s_doubled, 1)
                dve.wait_ge(s_doubled, g + 1)

            def pairs(g, slot, t):
                window = bass.AP(s, 1, [[T * (NF + ND), P], [NF + ND, T], [1, ND], [1, NF]])
                now = bass.ds(g * TT + t, 1)
                nc.vector.tensor_tensor(
                    z[:, slot, t:t + 1, 0:NPAIR].rearrange("p t (d i) -> p t d i", d=ND),
                    s[:, now, 0:NF].unsqueeze(2).broadcast_to((P, 1, ND, NF)),
                    window[:, now], ALU.mult).then_inc(z_made, 1)

            def zt_low(g, parity, c):
                dve.wait_ge(zt_hi_made, 3 * g + c + 1)
                part = slice(2 * c * NB, 2 * (c + 1) * NB)
                nc.vector.tensor_tensor(zt_lo[:, part], zt_ps[(3 * parity + c) % 2][:, :],
                                        zt_hi[:, part].bitcast(f32), ALU.subtract).then_inc(zt_lo_made, 1)

            def h1_low(g, c):
                dve.wait_ge(h1_hi_made, 2 * g + c + 1)
                part = slice(2 * c * NB, 2 * (c + 1) * NB)
                nc.vector.scalar_tensor_tensor(out=h1_lo[:, part], in0=h1_ps[c][:, :], scalar=0.0,
                                               in1=h1_hi[:, part].bitcast(f32),
                                               op0=ALU.max, op1=ALU.subtract).then_inc(h1_lo_made, 1)

            def step(g, parity, looking, more, uses):
                def keeps(first, last):
                    if looking:
                        for q in range(first, min(last, NQ)):
                            keep(AHEAD * NQ + g * NQ + q, q % 2, sel_ps, q % 2)

                nxt = 1 - parity
                keeps(0, 4)
                h1_low(g, 0)
                if more:
                    row_sums(g + 1, nxt, 0, uses)
                keeps(4, 5)
                if more:
                    row_sums(g + 1, nxt, 1, uses)
                    double(g + 1)
                keeps(5, 6)
                if more:
                    pairs(g + 1, nxt, 0)
                keeps(6, 7)
                if more:
                    pairs(g + 1, nxt, 1)
                keeps(7, 8)
                h1_low(g, 1)
                if more:
                    for c in range(3):
                        zt_low(g + 1, nxt, c)
                keeps(8, NQ)

            features()
            make_table(0)
            for q in range(NQ):
                if q + 1 < NQ:
                    make_table(q + 1)
                if q == 5:
                    dve.wait_ge(w1_hi_made, 1)
                    nc.vector.tensor_tensor(w1_lo[:, :, :], w1_raw[:, :, :], w1_hi[:, :, :].bitcast(f32),
                                            ALU.subtract).then_inc(w1_split, 1)
                    dve.wait_ge(w2_hi_made, 1)
                    nc.vector.tensor_tensor(w2_lo[:, :, :], w2_raw[:, :, :], w2_hi[:, :, :].bitcast(f32),
                                            ALU.subtract).then_inc(w2_split, 1)
                for e in range(AHEAD):
                    n = q * AHEAD + e
                    keep(n, n % A_RING, sel_banks[n % SEL_RING], n % SEL_RING)
            for t in range(TT):
                row_sums(0, 0, t, 1)
            double(0)
            for t in range(TT):
                pairs(0, 0, t)
            for c in range(3):
                zt_low(0, 0, c)
            with dve.Fori(0, LOOKING // 2) as i:
                for j in range(2):
                    step(2 * i + j, j, True, True, i + 1 + j)
            for g in range(LOOKING, STEPS):
                step(g, g % 2, False, g + 1 < STEPS, (g + 1) // 2 + 1)

        @block.scalar
        def _(act):
            def one_hot(n, bank_, slot, first_use=False):
                act.wait_ge(a_done, n + 1)
                if not first_use:
                    ring = A_RING if bank_ is not None else 2
                    act.wait_ge(kept_made, n - ring + 1)
                nc.scalar.activation(onehot[:, slot, :, :].rearrange("p a b -> p (a b)"),
                                     (bank_ if bank_ is not None else a_ps)[:, :],
                                     ACT.Relu).then_inc(onehot_made, 1)

            def looked(g, at, count):
                act.wait_ge(looked_done, count)
                nc.scalar.activation(s[:, bass.ds(g * TT, TT), NG:NF], s_view[:, at * TT:(at + 1) * TT, 0:F],
                                     ACT.Copy).then_inc(looked_made, 1)

            def dense_copy(g, slot):
                nc.scalar.activation(z[:, slot, :, NPAIR:NPAIR + NDENSE], dense_sb[:, bass.ds(g * TT, TT), :],
                                     ACT.Copy).then_inc(dense_copied, 1)

            def zt_high(g, parity):
                for c in range(3):
                    act.wait_ge(zt_done, 3 * g + c + 1)
                    nc.scalar.activation(zt_hi[:, 2 * c * NB:2 * (c + 1) * NB],
                                         zt_ps[(3 * parity + c) % 2][:, :], ACT.Copy).then_inc(zt_hi_made, 1)

            def h1_high(g, c):
                act.wait_ge(h1_done, 2 * g + c + 1)
                nc.scalar.activation(h1_hi[:, 2 * c * NB:2 * (c + 1) * NB], h1_ps[c][:, :],
                                     ACT.Relu).then_inc(h1_hi_made, 1)

            def step(g, parity, looking, more):
                def hots(*qs):
                    for q in qs:
                        if looking and q < NQ:
                            one_hot(AHEAD * NQ + g * NQ + q, None, q % 2)
                hots(0, 1, 2, 3)
                h1_high(g, 0)
                hots(4, 5, 6, 7)
                h1_high(g, 1)
                if more:
                    dense_copy(g + 1, 1 - parity)
                hots(8)
                if more:
                    zt_high(g + 1, 1 - parity)
                hots(*range(9, NQ))
                act.wait_ge(h2_done, g + 1)
                for m in range(M2):
                    nc.scalar.activation(h2[:, m, :], h2_ps[:, m * NB:(m + 1) * NB], ACT.Relu,
                                         bias=b2_sb[:, m:m + 1]).then_inc(h2_made, 1)
                act.wait_ge(y_done, g + 1)
                nc.scalar.activation(y[:, bass.ds(g * TT, TT)], h2_ps[:, 0:TT], ACT.Copy).then_inc(y_made, 1)
                if looking:
                    looked(g + AHEAD, 0, g + 2)

            act.wait_ge(coef_in, 16)
            nc.scalar.activation(coef_sb[0:KF, :, :, :].rearrange("p q a m -> p (q a m)"), coef_raw[0:KF, :],
                                 ACT.Copy).then_inc(coef_made, 1)
            for c in range(T // 4):
                act.wait_ge(featT_done, c + 1)
                nc.scalar.activation(featT[0:KF, c * 4 * P:(c + 1) * 4 * P], zt_ps[c % 2][0:KF, :],
                                     ACT.Copy).then_inc(featT_made, 1)
            for q in range(NQ):
                if q == 4:
                    act.wait_ge(w1_in, 16)
                    nc.scalar.activation(w1_hi[:, :, :], w1_raw[:, :, :], ACT.Copy).then_inc(w1_hi_made, 1)
                    act.wait_ge(w2_in, 16)
                    nc.scalar.activation(w2_hi[:, :, :], w2_raw[:, :, :], ACT.Copy).then_inc(w2_hi_made, 1)
                for e in range(AHEAD):
                    n = q * AHEAD + e
                    one_hot(n, a_banks[n % A_RING], n % A_RING, first_use=n < A_RING)
            for e in range(AHEAD):
                looked(e, e, 1)
            act.wait_ge(dense_in, 16)
            act.wait_ge(small_in, 32)
            dense_copy(0, 0)
            zt_high(0, 0)
            with act.Fori(0, LOOKING // 2) as i:
                for j in range(2):
                    step(2 * i + j, j, True, True)
            for g in range(LOOKING, STEPS):
                step(g, g % 2, False, g + 1 < STEPS)

        @block.tensor
        def _(pe):
            def select_inputs(q, g, bank_):
                for side in range(2):
                    last = nc.tensor.matmul(bank_[:, side * NB:(side + 1) * NB], coef_sb[0:KF, q, side, :],
                                            featT[0:KF, bass.ds(g * NB, NB)], start=True, stop=True)
                last.then_inc(a_done, 1)

            def select(q, a_slot, bank_):
                for half, part in enumerate((table_hi, table_lo)):
                    last = nc.tensor.matmul(bank_[:, 0:NB], part[:, q, :], onehot[:, a_slot, 0, :],
                                            start=(half == 0), stop=(half == 1))
                last.then_inc(sel_done, 1)

            def collect(q, at, slot):
                for t in range(TT):
                    ones, col = (ones4, FIRST[q]) if q < NS else (ones1, q - NS)
                    last = nc.tensor.matmul(s_view[:, at * TT + t, col:col + ones.shape[1]],
                                            kept[:, slot, t * P:(t + 1) * P], ones, start=True, stop=True)
                return last

            def transpose_z(g, parity, first=False):
                for c in range(3):
                    if not (first and c < 2):
                        pe.wait_ge(zt_lo_made, 3 * g + c - 1)
                    for k in range(2):
                        for t in range(TT):
                            last = nc.tensor.transpose(
                                zt_ps[(3 * parity + c) % 2][:, (k * TT + t) * P:(k * TT + t + 1) * P],
                                z[:, parity, t, (2 * c + k) * P:(2 * c + k + 1) * P], ident[:, :])
                    last.then_inc(zt_done, 1)

            def product(out_ap, lhs, rhs, n_chunks, chunks, m):
                terms = [(0, 0), (0, 1), (1, 0)]
                for k in chunks:
                    for a, b in terms:
                        last = nc.tensor.matmul(out_ap, lhs[a][:, k, m * P:(m + 1) * P],
                                                rhs[b][:, k * NB:(k + 1) * NB],
                                                start=(k == 0 and (a, b) == terms[0]),
                                                stop=(k == n_chunks - 1 and (a, b) == terms[-1]))
                return last

            def step(g, parity, looking, more):
                def look(q):
                    if not (looking and q < NQ):
                        return
                    n = AHEAD * NQ + g * NQ + q
                    pe.wait_ge(onehot_made, n + 1)
                    if q + 1 < NQ:
                        select_inputs(q + 1, g + AHEAD, a_ps)
                    if q > 0:
                        pe.wait_ge(kept_made, n)
                    select(q, q % 2, sel_ps)
                    if q > 0:
                        collect(q - 1, 0, (q - 1) % 2)

                if looking:
                    select_inputs(0, g + AHEAD, a_ps)
                pe.wait_ge(zt_lo_made, 3 * (g + 1))
                for m in range(M1):
                    for half in range(2):
                        last = product(h1_ps[m // 2][:, (m % 2) * NB:(m % 2 + 1) * NB], (w1_hi, w1_lo),
                                       (zt_hi, zt_lo), K1, range(3 * half, 3 * half + 3), m)
                        if m % 2 and half:
                            last.then_inc(h1_done, 1)
                        look(2 * m + half)
                if more:
                    pe.wait_ge(z_made, TT * (g + 2))
                    pe.wait_ge(dense_copied, g + 2)
                    transpose_z(g + 1, 1 - parity)
                look(8)
                pe.wait_ge(h1_lo_made, 2 * (g + 1))
                for m in range(M2):
                    last = product(h2_ps[:, m * NB:(m + 1) * NB], (w2_hi, w2_lo), (h1_hi, h1_lo), M1,
                                   range(M1), m)
                    if m == M2 - 1:
                        last.then_inc(h2_done, 1)
                    look(9 + m)
                if looking:
                    pe.wait_ge(kept_made, AHEAD * NQ + (g + 1) * NQ)
                    collect(NQ - 1, 0, (NQ - 1) % 2).then_inc(looked_done, 1)
                pe.wait_ge(h2_made, M2 * (g + 1))
                for t in range(TT):
                    for m in range(M2):
                        last = nc.tensor.matmul(h2_ps[:, t:t + 1], h2[:, m, t * P:(t + 1) * P],
                                                w3_sb[:, m:m + 1], start=(m == 0), stop=(m == M2 - 1))
                last.then_inc(y_done, 1)

            pe.wait_ge(ident_made, 1)
            pe.wait_ge(feat_made, 3)
            for c in range(T // 4):
                if c >= 2:
                    pe.wait_ge(featT_made, c - 1)
                for t in range(4):
                    last = nc.tensor.transpose(zt_ps[c % 2][0:KF, t * P:(t + 1) * P], feat[:, 4 * c + t, :],
                                               ident[:, :])
                last.then_inc(featT_done, 1)
            pe.wait_ge(featT_made, T // 4)
            pe.wait_ge(coef_made, 1)
            pe.wait_ge(const_in, 16)
            turns = [(q, e) for q in range(NQ) for e in range(AHEAD)]
            for n in range(2):
                select_inputs(turns[n][0], turns[n][1], a_banks[n % A_RING])
            for n, (q, e) in enumerate(turns):
                if n + 2 < len(turns):
                    if n + 2 >= A_RING:
                        pe.wait_ge(onehot_made, n + 3 - A_RING)
                    select_inputs(turns[n + 2][0], turns[n + 2][1], a_banks[(n + 2) % A_RING])
                pe.wait_ge(onehot_made, n + 1)
                if n >= SEL_RING:
                    pe.wait_ge(kept_made, n - SEL_RING + 1)
                if e == 0:
                    pe.wait_ge(table_split, q + 1)
                select(q, n % A_RING, sel_banks[n % SEL_RING])
                if n > 0:
                    pe.wait_ge(kept_made, n)
                    collect(turns[n - 1][0], turns[n - 1][1], (n - 1) % SEL_RING)
            pe.wait_ge(kept_made, len(turns))
            collect(NQ - 1, AHEAD - 1, (len(turns) - 1) % SEL_RING).then_inc(looked_done, 1)

            pe.wait_ge(pad_made, 2)
            pe.wait_ge(z_made, TT)
            pe.wait_ge(dense_copied, 1)
            transpose_z(0, 0, first=True)
            pe.wait_ge(w1_split, 1)
            pe.wait_ge(w2_split, 1)
            with pe.Fori(0, LOOKING // 2) as i:
                for j in range(2):
                    step(2 * i + j, j, True, True)
            for g in range(LOOKING, STEPS):
                step(g, g % 2, False, g + 1 < STEPS)


def pair_rows():
    number = {}
    for i in range(NF):
        for j in range(i + 1, NF):
            number[i, j] = len(number)
    found = []
    for d in range(1, ND + 1):
        for i in range(NF):
            a, b = ORDER[i], ORDER[(i + d) % NF]
            found.append(number[min(a, b), max(a, b)])
    return found


def coefficients():
    c = np.zeros((KF, NQ, 2, P), np.float32)

    def put(q, side, at, feature, p):
        c[side * F + feature, q, side, at] = 2 * p
        c[(2 + side) * F + feature, q, side, at] = -1
        c[4 * F, q, side, at] = 1 - p * p

    for q, group in enumerate(GROUPS):
        for j, (f, base) in enumerate(group):
            for v in range(-(-VOCAB[f] // SMALL_LOW)):
                put(q, 0, base + v, FIRST[q] + j, v)
            for v in range(SMALL_LOW):
                put(q, 1, j * SMALL_LOW + v, FIRST[q] + j, v)
    for x in range(N_BIG):
        for v in range(P):
            put(NS + x, 0, v, x, v - CENTRE[0])
        for v in range(BIG_COLS):
            put(NS + x, 1, v, x, v - CENTRE[1])
    return c.reshape(KF, -1)


def constants():
    blocks = np.zeros((P, NS, 4), np.float32)
    for q, group in enumerate(GROUPS):
        for j, (f, base) in enumerate(group):
            blocks[base:base + -(-VOCAB[f] // SMALL_LOW), q, j] = 1
    ones4 = np.zeros((P, 4), np.float32)
    for j in range(4):
        ones4[j * SMALL_LOW:(j + 1) * SMALL_LOW, j] = 1
    centre = np.zeros((P, 2 * F), np.float32)
    centre[:, 0:N_BIG] = CENTRE[0]
    centre[:, F:F + N_BIG] = CENTRE[1]
    return np.concatenate([blocks.reshape(P, -1), ones4, np.ones((P, 1), np.float32), centre], axis=1)


def kernel(**inputs):
    import concourse.bacc as bacc
    from concourse.bass_utils import run_bass_kernel_spmd as run

    nc = bacc.Bacc("TRN2", target_bir_lowering=False, num_devices=1)
    arrays = {}

    def put(name, a):
        a = np.ascontiguousarray(a)
        arrays[f"in_{name}"] = a
        return nc.dram_tensor(f"in_{name}", a.shape, mybir.dt.from_np(a.dtype), kind="ExternalInput").ap()

    w1 = np.asarray(inputs["W_top1"])
    laid = np.zeros((COLS, N1), w1.dtype)
    laid[:NPAIR] = w1[pair_rows()]
    laid[NPAIR:NPAIR + NDENSE] = w1[NPAIR:]
    laid[NPAIR + NDENSE] = np.asarray(inputs["b_top1"])
    small = np.zeros((NS, P, SMALL_LOW * D), np.float32)
    for q, group in enumerate(GROUPS):
        for f, base in group:
            flat = np.asarray(inputs[f"tbl_{f}"]).reshape(-1)
            small[q, base:].reshape(-1)[:flat.size] = flat
    big = np.zeros((N_BIG, P, BIG_COLS, D), np.float32)
    for x, f in enumerate(STREAMED):
        padded = np.zeros((BIG_COLS * BIG_LOW, D), np.float32)
        padded[:VOCAB[f]] = np.asarray(inputs[f"tbl_{f}"])
        big[x] = padded.reshape(BIG_COLS, BIG_LOW, D).transpose(1, 0, 2)
    args = [put("ids", np.asarray(inputs["ids"])[:, ORDER]), put("dense_ctx", inputs["dense_ctx"]),
            [put(f"tbl_{f}", inputs[f"tbl_{f}"]) for f in GATHERED],
            put("small", small), put("big", big.reshape(N_BIG, P, BIG_COLS * D)),
            put("coef", coefficients()), put("const", constants()),
            put("w1", laid), put("w2", inputs["W_top2"]),
            put("b2", np.asarray(inputs["b_top2"]).reshape(M2, P).T),
            put("w3", np.asarray(inputs["W_top3"]).reshape(M2, P).T)]
    out = nc.dram_tensor("out_0", (B, 1), mybir.dt.float32, kind="ExternalOutput").ap()
    build(nc, *args, out)
    r = run(nc, [arrays], core_ids=[0])
    return r.results[0]["out_0"]
```

```python
import numpy as np
import concourse.bass as bass
from concourse import mybir
from contextlib import ExitStack

P = 128
B = 2048
T = B // P
VOCAB = [1000, 1000, 12500, 1250, 12500, 125000, 125000, 12500, 12500, 1000, 125000, 1250, 1250,
         1000, 1250, 1250, 1000, 1000, 1250, 1000, 1250, 12500, 12500, 1000, 1000, 1250, 1000, 1250,
         1000, 12500, 1250, 1250, 1000, 1000, 1250, 1000, 1000, 1250, 1250]
NF = len(VOCAB)
D = 64
ND = NF // 2
NPAIR = NF * ND
NDENSE = 16
K1 = 6
COLS = K1 * P
N1 = 512
N2 = 256
M1 = N1 // P
M2 = N2 // P
TT = 2
NB = TT * P
STEPS = T // TT

AHEAD = 4
ROWS_PER_PIECE = 32
PIECE_SLOTS = 6
ON_SCALAR = {4: (6, 8), 7: (14, 12)}
ON_VECTOR = {0: (1, 0), 1: (1, 1), 4: (2, 0), 5: (2, 1), 8: (3, 0), 9: (3, 1), 16: (5, 0), 17: (5, 1),
             20: (6, 0), 21: (6, 1), 24: (8, 0), 25: (8, 1)}
STREAM = (0, 1, 2, 4, 3, 7, 5, 6, 8)
ROW_TURNS = {22: (0, 0), 23: (0, 1)}
A_RING = 2
HOT_RING = 4
SEL_RING = 3

SMALL_LOW = 32


def plan():
    gathered = sorted((f for f in range(NF) if VOCAB[f] > 1250), key=lambda f: VOCAB[f])
    left = sorted((f for f in range(NF) if VOCAB[f] <= 1250), key=lambda f: -VOCAB[f])
    groups = []
    while left:
        group, used = [], 0
        for f in list(left):
            need = -(-VOCAB[f] // SMALL_LOW)
            if len(group) < P // SMALL_LOW and used + need <= P:
                group.append((f, used))
                used += need
                left.remove(f)
        groups.append(group)
    return gathered, groups


GATHERED, GROUPS = plan()
NG = len(GATHERED)
NQ = len(GROUPS)
ORDER = GATHERED + [f for group in GROUPS for f, _ in group]
F = NF - NG
KF = 4 * F + 1
BASE = [sum(len(g) for g in GROUPS[:q]) for q in range(NQ)]
LANES = P // AHEAD
ONE_AT = P - 1
assert F <= LANES and BASE[-1] + 4 <= LANES


def build(nc, ids, dense, tables, small_rows, coef, const, w1, w2, b2, w3, rows_of_2, out):
    f32 = mybir.dt.float32
    f32r = mybir.dt.float32r
    i32 = mybir.dt.int32
    ALU = mybir.AluOpType
    ACT = mybir.ActivationFunctionType
    AX = mybir.AxisListType

    with ExitStack() as ctx:
        def sb(name, shape, dt=f32):
            return ctx.enter_context(nc.sbuf_tensor(name, shape, dt))

        def bank(name):
            return ctx.enter_context(nc.psum_tensor(name, [P, 2 * NB], f32))

        def sem(name):
            return ctx.enter_context(nc.semaphore(name))

        ids_sb = sb("ids_sb", [P, T, NF], i32)
        index = sb("index", [P, 2, TT, NG], i32)
        rows = sb("rows", [P, 2, TT, NG * D])
        digits = sb("digits", [P, T, 2 * F], i32)
        feat = sb("feat", [P, T, KF])
        featT = sb("featT", [P, T * P], f32r)
        coef_raw = sb("coef_raw", [P, NQ * 2 * P], mybir.dt.int16)
        coef_sb = sb("coef_sb", [P, NQ, 2, P], f32r)
        const_sb = sb("const_sb", [P, const.shape[1]])
        blocks = const_sb[:, 0:4 * NQ].rearrange("p (q j) -> p q j", j=4)
        windows = sb("windows", [P, 2 * P + 4])
        windows_r = sb("windows_r", [P, 2 * P + 4], f32r)
        looked_T = sb("looked_T", [P, NB])
        piece = sb("piece", [P, PIECE_SLOTS, ROWS_PER_PIECE * D])
        sums = sb("sums", [P, NQ, SMALL_LOW])
        table = sb("table", [P, NQ, P])
        table_hi, table_lo = sb("table_hi", [P, NQ, P], f32r), sb("table_lo", [P, NQ, P], f32r)
        onehot = sb("onehot", [P, HOT_RING, 2, NB], f32r)
        kept = sb("kept", [P, SEL_RING, NB])
        kept_parts = sb("kept_parts", [P, 2, 2, NB], f32r)
        s = sb("s", [P, T, NF + ND])
        z = sb("z", [P, 2, TT, COLS])
        dense_sb = sb("dense_sb", [P, T, NDENSE])
        ident = sb("ident", [P, P])
        w1_raw = [piece[:, slot, 0:K1 // 2 * N1].rearrange("p (k n) -> p k n", n=N1) for slot in (3, 4)]
        w2_raw = piece[:, 5, 0:M1 * N2].rearrange("p (k n) -> p k n", n=N2)
        w1_hi, w1_lo = sb("w1_hi", [P, K1, N1], f32r), sb("w1_lo", [P, K1, N1], f32r)
        w2_hi, w2_lo = sb("w2_hi", [P, M1, N2], f32r), sb("w2_lo", [P, M1, N2], f32r)
        b2_sb = sb("b2_sb", [P, M2])
        w3_sb = sb("w3_sb", [P, M2])
        b2_w3_rows = sb("b2_w3_rows", [P, 2, N2])
        h1_rows = sb("h1_rows", [P, TT, N1])
        h2_rows = sb("h2_rows", [P, 2, N2])
        zt_hi, zt_lo = sb("zt_hi", [P, K1 * NB], f32r), sb("zt_lo", [P, K1 * NB], f32r)
        h1_hi, h1_lo = sb("h1_hi", [P, M1 * NB], f32r), sb("h1_lo", [P, M1 * NB], f32r)
        h2 = sb("h2", [P, M2, NB])
        y = sb("y", [P, T])

        zt_ps = [bank("zt_ps0"), bank("zt_ps1")]
        h1_ps = [bank("h1_ps0"), bank("h1_ps1")]
        h2_ps = bank("h2_ps")
        a_ps = bank("a_ps")
        sel_ps = bank("sel_ps")
        s_ps = bank("s_ps")
        a_banks = [a_ps, h2_ps]
        sel_banks = [sel_ps, h1_ps[0], h1_ps[1]]
        looked_ps = s_ps[:, 0:NB]
        first_ps = zt_ps[0][0:LANES, 0:NB]
        back_first = zt_ps[1][:, 0:NB].rearrange("p (t e f) -> p t e f", t=TT, f=LANES)
        back_ps = s_ps[:, NB:2 * NB].rearrange("p (t e f) -> p t e f", t=TT, f=LANES)

        def slot_of(columns, t):
            return columns[:, :].rearrange("p (k t b) -> p k t b", k=2, t=TT)[:, :, t, :]

        last_h1_ps = h1_ps
        last_h1T_ps = s_ps[:, :].rearrange("p (k b) -> p k b", b=P)
        last_h2_ps = [sel_ps[:, 0:N2], zt_ps[1][:, 0:N2]]

        def h1_slot(h1, t):
            return h1[:, :].rearrange("p (k t b) -> p k t b", t=TT, b=P)[:, :, t, :]

        PAIR_PARTS = [(0, -(-2 * P // NF)), (-(-2 * P // NF), -(-4 * P // NF)), (-(-4 * P // NF), ND)]

        zt_banks = {(parity, c): zt_ps[(3 * parity + c) % 2] for parity in range(2) for c in range(3)}
        zt_banks["first", 2], zt_banks["last", 2] = h2_ps, a_ps
        for c in range(2):
            zt_banks["first", c] = zt_banks[0, c]
            zt_banks["last", c] = zt_banks[(STEPS - 1) % 2, c]
        featT_banks = [zt_ps[0], zt_ps[1], zt_ps[1], zt_ps[1]]

        first_ids_in = sem("first_ids_in")
        ids_in, const_in = sem("ids_in"), sem("const_in")
        coef_in = [sem("coef_in0"), sem("coef_in1")]
        w1_in = [sem("w1_in0"), sem("w1_in1")]
        piece_in = [sem(f"piece_in{n}") for n in range(PIECE_SLOTS)]
        dense_in, w2_in, small_in, y_out = sem("dense_in"), sem("w2_in"), sem("small_in"), sem("y_out")
        gathered_last = sem("gathered_last")
        gathered = [[sem(f"gathered{slot}_{t}") for t in range(TT)] for slot in range(2)]
        ident_zero, ident_made, pad_made, index_made = (sem("ident_zero"), sem("ident_made"),
                                                        sem("pad_made"), sem("index_made"))
        digits_made, feat_made, featT_done, featT_made = (sem("digits_made"), sem("feat_made"),
                                                          sem("featT_done"), sem("featT_made"))
        coef_made, ones_made = sem("coef_made"), sem("ones_made")
        windows_zero, windows_made = sem("windows_zero"), sem("windows_made")
        piece_summed, row_summed = sem("piece_summed"), sem("row_summed")
        table_made, table_hi_made, table_split = (sem("table_made"), sem("table_hi_made"),
                                                  sem("table_split"))
        a_done, onehot_made, sel_done, kept_made = (sem("a_done"), sem("onehot_made"), sem("sel_done"),
                                                    sem("kept_made"))
        looked_done, looked_copied = sem("looked_done"), sem("looked_copied")
        back_done, looked_made = sem("back_done"), sem("looked_made")
        summed, s_doubled, z_made, dense_copied = (sem("summed"), sem("s_doubled"), sem("z_made"),
                                                   sem("dense_copied"))
        w1_hi_made, w2_hi_made, w1_split, w2_split = (sem("w1_hi_made"), sem("w2_hi_made"),
                                                      sem("w1_split"), sem("w2_split"))
        zt_done, zt_hi_made, zt_lo_made = sem("zt_done"), sem("zt_hi_made"), sem("zt_lo_made")
        h1_done, h1_hi_made, h1_lo_made = sem("h1_done"), sem("h1_hi_made"), sem("h1_lo_made")
        last_h1_done, last_h1_made = sem("last_h1_done"), sem("last_h1_made")
        last_h1T_done, last_hi_made, last_lo_made = (sem("last_h1T_done"), sem("last_hi_made"),
                                                     sem("last_lo_made"))
        last_h2_done, last_h2_steps = sem("last_h2_done"), sem("last_h2_steps")
        h2_done, h2_made, y_done, y_made = sem("h2_done"), sem("h2_made"), sem("y_done"), sem("y_made")

        def piece_of(q):
            return STREAM.index(q)

        def summed_by_vector(n):
            return 2 * sum(q not in ON_SCALAR for q in STREAM[:n + 1])

        def summed_by_scalar(n):
            return SMALL_LOW * sum(q in ON_SCALAR for q in STREAM[:n + 1])

        LAST = NQ - 2
        turns = [(q, e) for q in range(LAST) for e in range(AHEAD)]
        turns += [(LAST, 0), (LAST, 1), (LAST + 1, 0), (LAST, 2), (LAST + 1, 1), (LAST, 3),
                  (LAST + 1, 2), (LAST + 1, 3)]
        FIRST_DONE = turns.index((LAST + 1, 0))

        def first_turn(q):
            return [of for of, _ in turns].index(q)

        def share(n, span, total):
            turn = n - span[0]
            if not 0 <= turn < span[1]:
                return range(0)
            return range(total * turn // span[1], total * (turn + 1) // span[1])

        FEATURES_TURN = 20
        W1_HIGH_TURN = 28
        W1_TURNS = range(30, 34)
        W1_HALF = K1 // 2
        COEF_FIRST = 2 * 2 * P
        LOOKING = STEPS - AHEAD

        block = ctx.enter_context(nc.Block())

        @block.sync
        def _(sp):
            ids_slots = ids.rearrange("(p t) f -> p t f", t=T)
            sp.dma_start(ids_sb[:, 0:TT, :], ids_slots[:, 0:TT, :]).then_inc(first_ids_in, 16)
            sp.dma_start(ids_sb[:, TT:T, :], ids_slots[:, TT:T, :]).then_inc(ids_in, 16)
            sp.dma_start(const_sb[:, :], const).then_inc(const_in, 16)
            def wait_summed(n):
                if STREAM[n] in ON_SCALAR:
                    sp.wait_ge(row_summed, summed_by_scalar(n))
                else:
                    sp.wait_ge(piece_summed, summed_by_vector(n))

            def last_in(slot):
                return max(n for n in range(NQ) if n % PIECE_SLOTS == slot)

            for n, q in enumerate(STREAM):
                if n == 0:
                    sp.dma_start(coef_raw[0:KF, 0:COEF_FIRST], coef[:, 0:COEF_FIRST]).then_inc(
                        coef_in[0], 16)
                if n == 1:
                    sp.dma_start(coef_raw[0:KF, COEF_FIRST:], coef[:, COEF_FIRST:]).then_inc(
                        coef_in[1], 16)
                if n >= PIECE_SLOTS:
                    wait_summed(n - PIECE_SLOTS)
                sp.dma_start(piece[:, n % PIECE_SLOTS, :], small_rows[q]).then_inc(
                    piece_in[n % PIECE_SLOTS], 16)
            w1_chunks = w1.rearrange("(k p) n -> p k n", p=P)
            for half in range(2):
                part = slice(half * K1 // 2, (half + 1) * K1 // 2)
                wait_summed(last_in(3 + half))
                sp.dma_start(w1_raw[half], w1_chunks[:, part, :]).then_inc(w1_in[half], 16)
            sp.dma_start(dense_sb[:, :, :], dense.rearrange("(p t) d -> p t d", t=T)).then_inc(dense_in, 16)
            wait_summed(last_in(5))
            sp.dma_start(w2_raw, w2.rearrange("(k p) n -> p k n", p=P)).then_inc(w2_in, 16)
            sp.dma_start(b2_sb[:, :], b2).then_inc(small_in, 16)
            sp.dma_start(w3_sb[:, :], w3).then_inc(small_in, 16)
            sp.dma_start(b2_w3_rows[:, :, :], rows_of_2).then_inc(small_in, 16)
            sp.wait_ge(y_made, STEPS - 1 + TT)
            sp.dma_start(out.rearrange("(p t) o -> p (t o)", t=T), y[:, :]).then_inc(y_out, 16)
            sp.wait_ge(y_out, 16)

        @block.gpsimd
        def _(pool):
            def gather(g, slot, last_step=False):
                nc.gpsimd.tensor_copy(index[:, slot, :, :],
                                      ids_sb[:, bass.ds(g * TT, TT), 0:NG]).then_inc(index_made, 1)
                pool.wait_ge(index_made, g + 1)
                pool.nop(nofuse=True)
                for t in range(TT):
                    for f in range(NG):
                        last = last_step and t == TT - 1 and f == NG - 1
                        nc.gpsimd.indirect_dma_start(
                            out=rows[:, slot, t, f * D:(f + 1) * D], out_offset=None, in_=tables[f],
                            in_offset=bass.IndirectOffsetOnAxis(ap=index[:, slot, t, f:f + 1], axis=0),
                        ).then_inc(gathered_last if last else gathered[slot][t], 16)

            nc.gpsimd.memset(ident[:, :], 0.0).then_inc(ident_zero, 1)
            pool.wait_ge(ident_zero, 1)
            nc.gpsimd.affine_select(out=ident[:, :], in_=ident[:, :], compare_op=ALU.not_equal, fill=1.0,
                                    base=0, pattern=[[-1, P]], channel_multiplier=1).then_inc(ident_made, 1)
            nc.gpsimd.memset(windows[:, :], 0.0).then_inc(windows_zero, 1)
            nc.gpsimd.memset(z[:, :, :, NPAIR + NDENSE:NPAIR + NDENSE + 1], 1.0).then_inc(pad_made, 1)
            nc.gpsimd.memset(z[:, :, :, NPAIR + NDENSE + 1:COLS], 0.0).then_inc(pad_made, 1)
            pool.wait_ge(first_ids_in, 16)
            gather(0, 0)
            pool.wait_ge(ids_in, 16)
            gather(1, 1)
            with pool.Fori(0, STEPS // 2 - 2) as i:
                for slot in range(2):
                    g = 2 * i + 2 + slot
                    pool.wait_ge(summed, TT * (g - 1))
                    gather(g, slot)
            for g in range(STEPS - 2, STEPS):
                pool.wait_ge(summed, TT * (g - 1))
                gather(g, g % 2, last_step=(g == STEPS - 1))

        @block.vector
        def _(dve):
            def make_digits():
                dve.wait_ge(first_ids_in, 16)
                dve.wait_ge(ids_in, 16)
                looked_up = ids_sb[:, :, NG:NF]
                nc.vector.tensor_scalar(digits[:, :, 0:F], looked_up, 5, None,
                                        ALU.logical_shift_right).then_inc(digits_made, 1)
                nc.vector.tensor_scalar(digits[:, :, F:2 * F], looked_up, SMALL_LOW - 1, None,
                                        ALU.bitwise_and).then_inc(digits_made, 1)
                dve.wait_ge(digits_made, 2)

            def features_of(half):
                now = slice(half * T // 2, (half + 1) * T // 2)
                nc.vector.tensor_copy(feat[:, now, 0:2 * F], digits[:, now, :]).then_inc(feat_made, 1)
                dve.wait_ge(feat_made, 2 + 2 * half)
                nc.vector.tensor_tensor(feat[:, now, 2 * F:4 * F], feat[:, now, 0:2 * F],
                                        feat[:, now, 0:2 * F], ALU.mult).then_inc(feat_made, 1)

            def sum_half(q, half):
                n = piece_of(q)
                dve.wait_ge(piece_in[n % PIECE_SLOTS], 16 * (n // PIECE_SLOTS + 1))
                now = slice(half * SMALL_LOW // 2, (half + 1) * SMALL_LOW // 2)
                nc.vector.tensor_reduce(
                    sums[:, q, now],
                    piece[:, n % PIECE_SLOTS, :].rearrange("p (r d) -> p r d", d=D)[:, now, :],
                    axis=AX.X, op=ALU.add).then_inc(piece_summed, 1)

            def place(q):
                if q in ON_SCALAR:
                    dve.wait_ge(row_summed, summed_by_scalar(piece_of(q)))
                else:
                    dve.wait_ge(piece_summed, summed_by_vector(piece_of(q)))
                nc.vector.tensor_tensor(
                    table[:, q, :].rearrange("p (j c) -> p j c", j=4),
                    sums[:, q, :].unsqueeze(1).broadcast_to((P, 4, SMALL_LOW)),
                    blocks[:, q, :].unsqueeze(2).broadcast_to((P, 4, SMALL_LOW)),
                    ALU.mult).then_inc(table_made, 1)

            def table_high(q):
                dve.wait_ge(table_made, q + 1)
                nc.vector.tensor_copy(table_hi[:, q, :], table[:, q, :]).then_inc(table_hi_made, 1)

            def table_low(q):
                dve.wait_ge(table_hi_made, q + 1)
                nc.vector.tensor_tensor(table_lo[:, q, :], table[:, q, :], table_hi[:, q, :].bitcast(f32),
                                        ALU.subtract).then_inc(table_split, 1)

            def keep(n):
                dve.wait_ge(sel_done, n + 1)
                nc.vector.tensor_tensor(kept[:, n % SEL_RING, :], onehot[:, n % HOT_RING, 1, :].bitcast(f32),
                                        sel_banks[n % SEL_RING][:, 0:NB], ALU.mult).then_inc(kept_made, 1)

            def keep_parts(n, slot):
                dve.wait_ge(sel_done, n + 1)
                nc.vector.tensor_tensor(kept_parts[:, slot, :, :],
                                        onehot[:, slot, 1:2, :].bitcast(f32).broadcast_to((P, 2, NB)),
                                        sel_ps[:, :].rearrange("p (h b) -> p h b", h=2),
                                        ALU.mult).then_inc(kept_made, 1)

            def sum_fields(g, slot, t, first, last):
                nc.vector.tensor_reduce(
                    s[:, bass.ds(g * TT + t, 1), first:last],
                    rows[:, slot, t, first * D:last * D].rearrange("p (o f d) -> p o f d", o=1, d=D),
                    axis=AX.X, op=ALU.add).then_inc(summed, 1)

            def row_sums(g, slot, t, uses, very_last=False):
                if very_last:
                    dve.wait_ge(gathered[slot][t], (NG * uses - 1) * 16)
                    sum_fields(g, slot, t, 0, NG - 1)
                    dve.wait_ge(gathered_last, 16)
                    sum_fields(g, slot, t, NG - 1, NG)
                else:
                    dve.wait_ge(gathered[slot][t], NG * 16 * uses)
                    sum_fields(g, slot, t, 0, NG)

            def double(g, looks, t=None):
                first, count, before = (g * TT, TT, g) if t is None else (g * TT + t, 1, g + t)
                dve.wait_ge(summed, TT * (g + 1) if t is None else TT * g + 2 * t + 1)
                dve.wait_ge(looked_made, TT * looks)
                nc.vector.tensor_copy(s[:, bass.ds(first, count), NF:NF + ND],
                                      s[:, bass.ds(first, count), 0:ND]).then_inc(s_doubled, 1)
                dve.wait_ge(s_doubled, before + 1)

            def pairs(g, slot, t, first=0, last=ND):
                window = bass.AP(s, 1, [[T * (NF + ND), P], [NF + ND, T], [1, ND], [1, NF]])
                now = bass.ds(g * TT + t, 1)
                nc.vector.tensor_tensor(
                    z[:, slot, t:t + 1, first * NF:last * NF].rearrange("p t (d i) -> p t d i", i=NF),
                    s[:, now, 0:NF].unsqueeze(2).broadcast_to((P, 1, last - first, NF)),
                    window[:, now, first:last, :], ALU.mult).then_inc(z_made, 1)

            def zt_low(g, banks, c):
                dve.wait_ge(zt_hi_made, 3 * g + c + 1)
                part = slice(2 * c * NB, 2 * (c + 1) * NB)
                nc.vector.tensor_tensor(zt_lo[:, part], zt_banks[banks, c][:, :],
                                        zt_hi[:, part].bitcast(f32), ALU.subtract).then_inc(zt_lo_made, 1)

            def zt_low_of(t):
                for c in range(3):
                    dve.wait_ge(zt_hi_made, 3 * (STEPS - 1) + 3 * t + c + 1)
                    nc.vector.tensor_tensor(
                        slot_of(zt_lo[:, 2 * c * NB:2 * (c + 1) * NB], t), slot_of(zt_banks["last", c], t),
                        slot_of(zt_hi[:, 2 * c * NB:2 * (c + 1) * NB], t).bitcast(f32),
                        ALU.subtract).then_inc(zt_lo_made, 1)

            def h1_low(g, c):
                dve.wait_ge(h1_hi_made, 2 * g + c + 1)
                part = slice(2 * c * NB, 2 * (c + 1) * NB)
                nc.vector.scalar_tensor_tensor(out=h1_lo[:, part], in0=h1_ps[c][:, :], scalar=0.0,
                                               in1=h1_hi[:, part].bitcast(f32),
                                               op0=ALU.max, op1=ALU.subtract).then_inc(h1_lo_made, 1)

            def last_h1_low(t):
                dve.wait_ge(last_hi_made, t + 1)
                nc.vector.tensor_tensor(h1_slot(h1_lo, t), last_h1T_ps, h1_slot(h1_hi, t).bitcast(f32),
                                        ALU.subtract).then_inc(last_lo_made, 1)

            def last_y(t):
                dve.wait_ge(last_h2_done, t + 1)
                nc.vector.tensor_tensor(h2_rows[:, 0, :], last_h2_ps[t], b2_w3_rows[:, 0, :],
                                        ALU.add).then_inc(last_h2_steps, 1)
                dve.wait_ge(last_h2_steps, 2 * t + 1)
                nc.vector.scalar_tensor_tensor(out=h2_rows[:, 1, :], in0=h2_rows[:, 0, :], scalar=0.0,
                                               in1=b2_w3_rows[:, 1, :], op0=ALU.max,
                                               op1=ALU.mult).then_inc(last_h2_steps, 1)
                dve.wait_ge(last_h2_steps, 2 * t + 2)
                at = (STEPS - 1) * TT + t
                nc.vector.tensor_reduce(y[:, at:at + 1], h2_rows[:, 1, :], axis=AX.X,
                                        op=ALU.add).then_inc(y_made, 1)

            def step(g, parity, looking, uses, looks):
                def keeps(first, last):
                    if looking:
                        for q in range(first, last):
                            keep_parts(AHEAD * NQ + g * NQ + q, (q + parity * NQ) % 2)

                more = looking or g + 1 < STEPS
                late = not looking and g + 2 == STEPS
                nxt = 1 - parity
                again = uses + parity - 1
                if more and not late:
                    row_sums(g + 1, nxt, 0, again)
                if looking:
                    row_sums(g + 1, nxt, 1, again)
                keeps(0, 2)
                h1_low(g, 0)
                if late:
                    row_sums(g + 1, nxt, 0, again)
                    double(g + 1, looks, 0)
                    pairs(g + 1, nxt, 0)
                    h1_low(g, 1)
                    zt_low_of(0)
                    row_sums(g + 1, nxt, 1, again, very_last=True)
                    double(g + 1, looks, 1)
                    for first, last in PAIR_PARTS:
                        pairs(g + 1, nxt, 1, first, last)
                    zt_low_of(1)
                    for t in range(TT):
                        last_h1_low(t)
                        if t > 0:
                            dve.wait_ge(small_in, 48)
                            last_y(t - 1)
                    last_y(TT - 1)
                    return
                if more and not looking:
                    row_sums(g + 1, nxt, 1, again)
                if more:
                    double(g + 1, looks)
                    keeps(2, 3)
                    pairs(g + 1, nxt, 0)
                    keeps(3, 4)
                    pairs(g + 1, nxt, 1)
                keeps(4, 6)
                h1_low(g, 1)
                keeps(6, 7)
                if more:
                    zt_low(g + 1, nxt, 0)
                keeps(7, 8)
                if more:
                    zt_low(g + 1, nxt, 1)
                keeps(8, NQ)
                if more:
                    zt_low(g + 1, nxt, 2)

            def w1_low(c):
                dve.wait_ge(w1_hi_made, c + 1)
                nc.vector.tensor_tensor(w1_lo[:, c, :], w1_raw[c // W1_HALF][:, c % W1_HALF, :],
                                        w1_hi[:, c, :].bitcast(f32), ALU.subtract).then_inc(w1_split, 1)

            nc.vector.memset(feat[:, :, 4 * F:KF], 1.0).then_inc(feat_made, 1)
            make_digits()
            features_of(0)
            for half in range(2):
                sum_half(0, half)
            dve.wait_ge(const_in, 16)
            place(0)
            table_high(0)
            table_low(0)
            features_of(1)
            dve.wait_ge(windows_zero, 1)
            nc.vector.tensor_copy(windows[:, ONE_AT:ONE_AT + 4],
                                  const_sb[:, 4 * NQ:4 * NQ + 4]).then_inc(ones_made, 1)
            for n, (q, e) in enumerate(turns[:FIRST_DONE + 1]):
                ahead = q + 1
                if n in ON_VECTOR:
                    sum_half(*ON_VECTOR[n])
                if ahead < NQ:
                    if n == first_turn(ahead) - 2:
                        place(ahead)
                    if n == first_turn(ahead) - 1:
                        table_high(ahead)
                        table_low(ahead)
                if n in ROW_TURNS:
                    g, t = ROW_TURNS[n]
                    row_sums(g, g, t, 1)
                if n in W1_TURNS:
                    w1_low(n - W1_TURNS[0])
                keep(n)
            for n in range(FIRST_DONE + 1, FIRST_DONE + 4):
                if n in W1_TURNS:
                    w1_low(n - W1_TURNS[0])
                keep(n)
            double(0, 1)
            for t in range(TT):
                pairs(0, 0, t)
            for n in range(FIRST_DONE + 4, len(turns)):
                keep(n)
            zt_low(0, "first", 0)
            zt_low(0, "first", 1)
            for c in range(len(W1_TURNS), K1):
                w1_low(c)
            zt_low(0, "first", 2)
            dve.wait_ge(w2_hi_made, 1)
            nc.vector.tensor_tensor(w2_lo[:, :, :], w2_raw, w2_hi[:, :, :].bitcast(f32),
                                    ALU.subtract).then_inc(w2_split, 1)
            with dve.Fori(0, LOOKING // 2) as i:
                for j in range(2):
                    step(2 * i + j, j, True, i + 2, 2 * i + j + 2)
            for g in range(LOOKING, STEPS - 1):
                step(g, g % 2, False, g // 2 + 2, min(g, LOOKING) + 2)

        @block.scalar
        def _(act):
            def one_hot(n, bank_, slot):
                act.wait_ge(a_done, n + 1)
                nc.scalar.activation(onehot[:, slot, :, :].rearrange("p a b -> p (a b)"), bank_[:, :],
                                     ACT.Relu).then_inc(onehot_made, 1)

            def copy_looked(source, lanes, count):
                act.wait_ge(looked_done, count)
                nc.scalar.activation(looked_T[0:lanes, :], source, ACT.Copy).then_inc(looked_copied, 1)

            def place_looked(g, source, lane, steps, count):
                act.wait_ge(back_done, count)
                for t in range(TT):
                    nc.scalar.activation(
                        s[:, bass.ds(g * TT, steps * TT), NG:NF].rearrange(
                            "p (e t) f -> p e t f", t=TT)[:, :, t, :],
                        source[:, t, lane:lane + steps, 0:F], ACT.Copy).then_inc(looked_made, 1)

            def w1_high(c):
                act.wait_ge(w1_in[c // W1_HALF], 16)
                nc.scalar.activation(w1_hi[:, c, :], w1_raw[c // W1_HALF][:, c % W1_HALF, :],
                                     ACT.Copy).then_inc(w1_hi_made, 1)

            def coefs(first, last, half):
                act.wait_ge(coef_in[half], 16)
                nc.scalar.activation(coef_sb[0:KF, :, :, :].rearrange("p q a m -> p (q a m)")[:, first:last],
                                     coef_raw[0:KF, first:last], ACT.Copy).then_inc(coef_made, 1)

            def feature_copy(c):
                act.wait_ge(featT_done, c + 1)
                nc.scalar.activation(featT[0:KF, c * 4 * P:(c + 1) * 4 * P], featT_banks[c][0:KF, :],
                                     ACT.Copy).then_inc(featT_made, 1)

            def sum_rows(q, rows_):
                slot = piece_of(q) % PIECE_SLOTS
                act.wait_ge(piece_in[slot], 16 * (piece_of(q) // PIECE_SLOTS + 1))
                for row in rows_:
                    there = piece[:, slot, row * D:(row + 1) * D]
                    nc.scalar.activation(there, there, ACT.Copy,
                                         accum_out=sums[:, q, row:row + 1]).then_inc(row_summed, 1)

            def dense_copy(g, slot):
                nc.scalar.activation(z[:, slot, :, NPAIR:NPAIR + NDENSE], dense_sb[:, bass.ds(g * TT, TT), :],
                                     ACT.Copy).then_inc(dense_copied, 1)

            def zt_high(g, banks, c):
                act.wait_ge(zt_done, 3 * g + c + 1)
                nc.scalar.activation(zt_hi[:, 2 * c * NB:2 * (c + 1) * NB],
                                     zt_banks[banks, c][:, :], ACT.Copy).then_inc(zt_hi_made, 1)

            def zt_high_of(t):
                for c in range(3):
                    act.wait_ge(zt_done, 3 * (STEPS - 1) + 3 * t + c + 1)
                    nc.scalar.activation(slot_of(zt_hi[:, 2 * c * NB:2 * (c + 1) * NB], t),
                                         slot_of(zt_banks["last", c], t), ACT.Copy).then_inc(zt_hi_made, 1)

            def h1_high(g, c):
                act.wait_ge(h1_done, 2 * g + c + 1)
                nc.scalar.activation(h1_hi[:, 2 * c * NB:2 * (c + 1) * NB], h1_ps[c][:, :],
                                     ACT.Relu).then_inc(h1_hi_made, 1)

            def step(g, parity, looking, more):
                def hots(first, last):
                    if looking:
                        for q in range(first, last):
                            n = AHEAD * NQ + g * NQ + q
                            act.wait_ge(kept_made, n - 1)
                            one_hot(n, a_ps, (q + parity * NQ) % 2)

                late = not looking and g + 2 == STEPS
                hots(0, 2)
                h1_high(g, 0)
                if more:
                    dense_copy(g + 1, 1 - parity)
                hots(2, 6)
                h1_high(g, 1)
                if late:
                    zt_high_of(0)
                hots(6, 7)
                if more and not late:
                    zt_high(g + 1, 1 - parity, 0)
                hots(7, 8)
                if more and not late:
                    zt_high(g + 1, 1 - parity, 1)
                hots(8, NQ)
                if more and not late:
                    zt_high(g + 1, 1 - parity, 2)
                if looking:
                    copy_looked(looked_ps[0:LANES, :], LANES, g + 3)
                act.wait_ge(h2_done, g + 1)
                apart = late
                for m in range(M2):
                    from_ = sel_ps[:, 0:NB] if apart and m else h2_ps[:, m * NB:(m + 1) * NB]
                    nc.scalar.activation(h2[:, m, :], from_, ACT.Relu,
                                         bias=b2_sb[:, m:m + 1]).then_inc(h2_made, 1)
                if looking:
                    place_looked(g + AHEAD, back_ps, 0, 1, g + 3)
                if late:
                    zt_high_of(1)
                    for t in range(TT):
                        act.wait_ge(last_h1_done, t + 1)
                        nc.scalar.activation(h1_rows[:, t, :], last_h1_ps[t][:, :], ACT.Relu).then_inc(
                            last_h1_made, 1)
                        act.wait_ge(last_h1T_done, t + 1)
                        nc.scalar.activation(h1_slot(h1_hi, t), last_h1T_ps, ACT.Copy).then_inc(
                            last_hi_made, 1)
                act.wait_ge(y_done, g + 1)
                nc.scalar.activation(y[:, bass.ds(g * TT, TT)], h2_ps[:, 0:TT], ACT.Copy).then_inc(y_made, 1)

            feature_copy(0)
            coefs(0, COEF_FIRST, 0)
            feature_copy(1)
            for n, (q, e) in enumerate(turns):
                if n == 1:
                    coefs(COEF_FIRST, NQ * 2 * P, 1)
                if n == 2:
                    act.wait_ge(ones_made, 1)
                    nc.scalar.activation(windows_r[:, :], windows[:, :],
                                         ACT.Copy).then_inc(windows_made, 1)
                if n >= HOT_RING:
                    act.wait_ge(kept_made, n - HOT_RING + 1)
                one_hot(n, a_banks[n % A_RING], n % HOT_RING)
                if n in (3, FEATURES_TURN + 3):
                    feature_copy(2 if n == 3 else 3)
                if 0 <= n - W1_HIGH_TURN < K1:
                    w1_high(n - W1_HIGH_TURN)
                if n == FIRST_DONE + 4:
                    copy_looked(first_ps, LANES, 1)
                for summed_group, span in ON_SCALAR.items():
                    rows_ = share(n, span, SMALL_LOW)
                    if rows_:
                        sum_rows(summed_group, rows_)
            place_looked(0, back_first, 0, 1, 1)
            act.wait_ge(dense_in, 16)
            dense_copy(0, 0)
            zt_high(0, "first", 0)
            zt_high(0, "first", 1)
            copy_looked(looked_ps, P, 2)
            act.wait_ge(w2_in, 16)
            nc.scalar.activation(w2_hi[:, :, :], w2_raw, ACT.Copy).then_inc(w2_hi_made, 1)
            zt_high(0, "first", 2)
            place_looked(1, back_ps, 1, AHEAD - 1, 2)
            act.wait_ge(small_in, 48)
            with act.Fori(0, LOOKING // 2) as i:
                for j in range(2):
                    step(2 * i + j, j, True, True)
            for g in range(LOOKING, STEPS - 1):
                step(g, g % 2, False, g + 1 < STEPS)

        @block.tensor
        def _(pe):
            def select_inputs(q, g, bank_):
                for side in range(2):
                    last = nc.tensor.matmul(bank_[:, side * NB:(side + 1) * NB], coef_sb[0:KF, q, side, :],
                                            featT[0:KF, bass.ds(g * NB, NB)], start=True, stop=True)
                last.then_inc(a_done, 1)

            def select(n, q):
                for half, part in enumerate((table_hi, table_lo)):
                    last = nc.tensor.matmul(sel_banks[n % SEL_RING][:, 0:NB], part[:, q, :],
                                            onehot[:, n % HOT_RING, 0, :], start=(half == 0), stop=(half == 1))
                last.then_inc(sel_done, 1)

            def select_parts(q, slot):
                for half, part in enumerate((table_hi, table_lo)):
                    last = nc.tensor.matmul(sel_ps[:, half * NB:(half + 1) * NB], part[:, q, :],
                                            onehot[:, slot, 0, :], start=True, stop=True)
                last.then_inc(sel_done, 1)

            def window(q, values, lane, lanes):
                first = ONE_AT - BASE[q] - lane
                return values[:, first:first + lanes]

            def collect(n, q, e):
                of_first = [n for n, (_, e) in enumerate(turns) if e == 0]
                of_others = [n for n, (_, e) in enumerate(turns) if e > 0]
                numbers, to, lane, lanes = ((of_first, first_ps, 0, LANES) if e == 0 else
                                            (of_others, looked_ps, e * LANES, P))
                last = nc.tensor.matmul(to, window(q, windows, lane, lanes), kept[:, n % SEL_RING, :],
                                        start=(n == numbers[0]), stop=(n == numbers[-1]))
                if n == numbers[-1]:
                    last.then_inc(looked_done, 1)

            def collect_parts(q, slot):
                for half in range(2):
                    last = nc.tensor.matmul(looked_ps[0:LANES, :], window(q, windows_r, 0, LANES),
                                            kept_parts[:, slot, half, :], start=(q == 0 and half == 0),
                                            stop=(q == NQ - 1 and half == 1))
                return last

            def turn_back(target, count):
                pe.wait_ge(looked_copied, count)
                for t in range(TT):
                    last = nc.tensor.transpose(target[:, t, :, :].rearrange("p e f -> p (e f)"),
                                               looked_T[:, t * P:(t + 1) * P], ident[:, :])
                last.then_inc(back_done, 1)

            def turn_first():
                pe.wait_ge(looked_copied, 1)
                for t in range(TT):
                    last = nc.tensor.transpose(zt_ps[1][:, t * P:t * P + LANES],
                                               looked_T[0:LANES, t * P:(t + 1) * P],
                                               ident[0:LANES, 0:LANES])
                last.then_inc(back_done, 1)

            def transpose_z(g, parity, c, banks):
                if banks == parity:
                    pe.wait_ge(zt_lo_made, 3 * g + c - 1)
                for k in range(2):
                    for t in range(TT):
                        last = nc.tensor.transpose(
                            zt_banks[banks, c][:, (k * TT + t) * P:(k * TT + t + 1) * P],
                            z[:, parity, t, (2 * c + k) * P:(2 * c + k + 1) * P], ident[:, :])
                last.then_inc(zt_done, 1)

            def transpose_z_of(t):
                g, parity = STEPS - 1, (STEPS - 1) % 2
                pe.wait_ge(dense_copied, g + 1)
                for c in range(3):
                    pe.wait_ge(z_made, TT * g + 1 + (c + 1) * t)
                    pe.wait_ge(zt_lo_made, 3 * g + (c + 1) * t)
                    for k in range(2):
                        last = nc.tensor.transpose(
                            zt_banks["last", c][:, (k * TT + t) * P:(k * TT + t + 1) * P],
                            z[:, parity, t, (2 * c + k) * P:(2 * c + k + 1) * P], ident[:, :])
                    last.then_inc(zt_done, 1)

            def product(out_ap, lhs, rhs, n_chunks, chunks, m):
                terms = [(0, 0), (0, 1), (1, 0)]
                for k in chunks:
                    for a, b in terms:
                        last = nc.tensor.matmul(out_ap, lhs[a][:, k, m * P:(m + 1) * P],
                                                rhs[b][:, k * NB:(k + 1) * NB],
                                                start=(k == 0 and (a, b) == terms[0]),
                                                stop=(k == n_chunks - 1 and (a, b) == terms[-1]))
                return last

            def first_layer(m, half):
                last = product(h1_ps[m // 2][:, (m % 2) * NB:(m % 2 + 1) * NB], (w1_hi, w1_lo),
                               (zt_hi, zt_lo), K1, range(3 * half, 3 * half + 3), m)
                if m % 2 and half:
                    last.then_inc(h1_done, 1)

            def second_layer(m, half, apart=False):
                to = sel_ps[:, 0:NB] if apart and m else h2_ps[:, m * NB:(m + 1) * NB]
                last = product(to, (w2_hi, w2_lo), (h1_hi, h1_lo), M1,
                               range(2 * half, 2 * half + 2), m)
                if m == M2 - 1 and half:
                    last.then_inc(h2_done, 1)

            def head(g):
                out_ap = h1_ps[0][:, 0:NB]
                pe.wait_ge(zt_lo_made, 3 * g + 1)
                product(out_ap, (w1_hi, w1_lo), (zt_hi, zt_lo), K1, range(0, 2), 0)
                pe.wait_ge(zt_lo_made, 3 * g + 2)
                product(out_ap, (w1_hi, w1_lo), (zt_hi, zt_lo), K1, range(2, 3), 0)

            def by_rows(out_ap, lhs, rhs, n_chunks, chunks, t):
                terms = [(0, 0), (0, 1), (1, 0)]
                for k in chunks:
                    for a, b in terms:
                        last = nc.tensor.matmul(out_ap, lhs[a][:, k * NB + t * P:k * NB + (t + 1) * P],
                                                rhs[b][:, k, :], start=(k == 0 and (a, b) == terms[0]),
                                                stop=(k == n_chunks - 1 and (a, b) == terms[-1]))
                return last

            def last_first_layer(t, chunks):
                pe.wait_ge(zt_lo_made, 3 * (STEPS - 1) + 3 * t + chunks[-1] // 2 + 1)
                last = by_rows(last_h1_ps[t][:, :], (zt_hi, zt_lo), (w1_hi, w1_lo), K1, chunks, t)
                if chunks[-1] == K1 - 1:
                    last.then_inc(last_h1_done, 1)

            def last_turn(t):
                pe.wait_ge(last_h1_made, t + 1)
                if t > 0:
                    pe.wait_ge(last_lo_made, t)
                for k in range(M1):
                    last = nc.tensor.transpose(last_h1T_ps[:, k, :], h1_rows[:, t, k * P:(k + 1) * P],
                                               ident[:, :])
                last.then_inc(last_h1T_done, 1)

            def last_second_layer(t):
                pe.wait_ge(last_lo_made, t + 1)
                by_rows(last_h2_ps[t], (h1_hi, h1_lo), (w2_hi, w2_lo), M1, range(M1), t).then_inc(
                    last_h2_done, 1)

            def step(g, parity, looking, more):
                def look(q):
                    if not looking:
                        return
                    n = AHEAD * NQ + g * NQ + q
                    pe.wait_ge(onehot_made, n + 1)
                    if q + 1 < NQ:
                        select_inputs(q + 1, g + AHEAD, a_ps)
                    if q > 0:
                        pe.wait_ge(kept_made, n)
                    select_parts(q, (q + parity * NQ) % 2)
                    if q == 1:
                        pe.wait_ge(looked_made, TT * (g + 2))
                    if q > 0:
                        collect_parts(q - 1, (q - 1 + parity * NQ) % 2)

                nxt = 1 - parity
                if looking:
                    select_inputs(0, g + AHEAD, a_ps)
                pe.wait_ge(w1_split, K1)
                pe.wait_ge(zt_lo_made, 3 * (g + 1))
                for n in range(1, 2 * M1):
                    first_layer(n // 2, n % 2)
                    if n > 1:
                        look(n - 2)
                late = not looking and g + 2 == STEPS
                apart = late
                if more and not late:
                    pe.wait_ge(z_made, TT * (g + 2))
                    pe.wait_ge(dense_copied, g + 2)
                    transpose_z(g + 1, nxt, 0, nxt)
                    transpose_z(g + 1, nxt, 1, nxt)
                look(6)
                pe.wait_ge(w2_split, 1)
                pe.wait_ge(h1_lo_made, 2 * g + 1)
                second_layer(0, 0)
                if apart:
                    second_layer(1, 0, apart)
                if late:
                    transpose_z_of(0)
                look(7)
                pe.wait_ge(h1_lo_made, 2 * (g + 1))
                second_layer(0, 1)
                look(8)
                if more and not late:
                    transpose_z(g + 1, nxt, 2, nxt)
                if not apart:
                    second_layer(1, 0)
                if looking:
                    pe.wait_ge(kept_made, AHEAD * NQ + (g + 1) * NQ)
                    collect_parts(NQ - 1, (NQ - 1 + parity * NQ) % 2).then_inc(looked_done, 1)
                second_layer(1, 1, apart)
                if more and not late:
                    head(g + 1)
                if looking:
                    turn_back(back_ps, g + 3)
                if late:
                    last_first_layer(0, range(0, 4))
                    transpose_z_of(1)
                    last_first_layer(0, range(4, K1))
                    last_first_layer(1, range(0, 3))
                    last_turn(0)
                    last_first_layer(1, range(3, K1))
                    pe.wait_ge(h2_made, M2 * (STEPS - 1))
                    last_second_layer(0)
                    last_turn(1)
                pe.wait_ge(h2_made, M2 * (g + 1))
                for t in range(TT):
                    for m in range(M2):
                        last = nc.tensor.matmul(h2_ps[:, t:t + 1], h2[:, m, t * P:(t + 1) * P],
                                                w3_sb[:, m:m + 1], start=(m == 0), stop=(m == M2 - 1))
                last.then_inc(y_done, 1)
                if late:
                    last_second_layer(1)

            def turn_features(c):
                pe.wait_ge(feat_made, 3 if c < 2 else 5)
                if c == 3:
                    pe.wait_ge(featT_made, 3)
                for t in range(4):
                    last = nc.tensor.transpose(featT_banks[c][0:KF, t * P:(t + 1) * P],
                                               feat[:, 4 * c + t, :], ident[:, :])
                last.then_inc(featT_done, 1)

            pe.wait_ge(ident_made, 1)
            turn_features(0)
            turn_features(1)
            pe.wait_ge(featT_made, 2)
            pe.wait_ge(coef_made, 1)
            for n in range(A_RING):
                select_inputs(*turns[n], a_banks[n])
            for n, (q, e) in enumerate(turns):
                pe.wait_ge(onehot_made, n + 1)
                later = n + A_RING
                if later < len(turns):
                    if turns[later][0] == 2 and turns[later][1] == 0:
                        pe.wait_ge(coef_made, 2)
                    select_inputs(*turns[later], a_banks[later % A_RING])
                if n == FIRST_DONE + 4:
                    pe.wait_ge(featT_made, 4)
                    turn_first()
                if n >= SEL_RING:
                    pe.wait_ge(kept_made, n - SEL_RING + 1)
                if n == first_turn(q):
                    pe.wait_ge(table_split, q + 1)
                select(n, q)
                if n in (0, FEATURES_TURN):
                    turn_features(2 if n == 0 else 3)
                if n == 2:
                    pe.wait_ge(ones_made, 1)
                    pe.wait_ge(const_in, 16)
                if n >= 2:
                    pe.wait_ge(kept_made, n - 1)
                    collect(n - 2, *turns[n - 2])
            pe.wait_ge(pad_made, 2)
            pe.wait_ge(z_made, TT)
            pe.wait_ge(dense_copied, 1)
            pe.wait_ge(onehot_made, len(turns))
            for c in range(3):
                transpose_z(0, 0, c, "first")
            for n in range(len(turns) - 2, len(turns)):
                pe.wait_ge(kept_made, n + 1)
                collect(n, *turns[n])
            pe.wait_ge(w1_split, W1_HALF)
            head(0)
            turn_back(back_ps, 2)
            pe.wait_ge(windows_made, 1)
            with pe.Fori(0, LOOKING // 2) as i:
                for j in range(2):
                    step(2 * i + j, j, True, True)
            for g in range(LOOKING, STEPS - 1):
                step(g, g % 2, False, g + 1 < STEPS)


def pair_rows():
    number = {}
    for i in range(NF):
        for j in range(i + 1, NF):
            number[i, j] = len(number)
    found = []
    for d in range(1, ND + 1):
        for i in range(NF):
            a, b = ORDER[i], ORDER[(i + d) % NF]
            found.append(number[min(a, b), max(a, b)])
    return found


def coefficients():
    c = np.zeros((KF, NQ, 2, P), np.int16)

    def put(q, side, at, feature, p):
        c[side * F + feature, q, side, at] = 2 * p
        c[(2 + side) * F + feature, q, side, at] = -1
        c[4 * F, q, side, at] = 1 - p * p

    feature = 0
    for q, group in enumerate(GROUPS):
        for j, (f, base) in enumerate(group):
            for v in range(-(-VOCAB[f] // SMALL_LOW)):
                put(q, 0, base + v, feature, v)
            for v in range(SMALL_LOW):
                put(q, 1, j * SMALL_LOW + v, feature, v)
            feature += 1
    return c.reshape(KF, -1)


def constants():
    blocks = np.zeros((P, NQ, 4), np.float32)
    for q, group in enumerate(GROUPS):
        for j, (f, base) in enumerate(group):
            blocks[base:base + -(-VOCAB[f] // SMALL_LOW), q, j] = 1
    ones4 = np.zeros((P, 4), np.float32)
    for j in range(4):
        ones4[j * SMALL_LOW:(j + 1) * SMALL_LOW, j] = 1
    return np.concatenate([blocks.reshape(P, -1), ones4], axis=1)


def kernel(**inputs):
    import concourse.bacc as bacc
    from concourse.bass_utils import run_bass_kernel_spmd as run

    nc = bacc.Bacc("TRN2", target_bir_lowering=False, num_devices=1)
    arrays = {}

    def put(name, a):
        a = np.ascontiguousarray(a)
        arrays[f"in_{name}"] = a
        return nc.dram_tensor(f"in_{name}", a.shape, mybir.dt.from_np(a.dtype), kind="ExternalInput").ap()

    w1 = np.asarray(inputs["W_top1"])
    laid = np.zeros((COLS, N1), w1.dtype)
    laid[:NPAIR] = w1[pair_rows()]
    laid[NPAIR:NPAIR + NDENSE] = w1[NPAIR:]
    laid[NPAIR + NDENSE] = np.asarray(inputs["b_top1"])
    small = np.zeros((NQ, P, SMALL_LOW * D), np.float32)
    for q, group in enumerate(GROUPS):
        for f, base in group:
            flat = np.asarray(inputs[f"tbl_{f}"]).reshape(-1)
            small[q, base:].reshape(-1)[:flat.size] = flat
    args = [put("ids", np.asarray(inputs["ids"])[:, ORDER]), put("dense_ctx", inputs["dense_ctx"]),
            [put(f"tbl_{f}", inputs[f"tbl_{f}"]) for f in GATHERED],
            put("small", small),
            put("coef", coefficients()), put("const", constants()),
            put("w1", laid), put("w2", inputs["W_top2"]),
            put("b2", np.asarray(inputs["b_top2"]).reshape(M2, P).T),
            put("w3", np.asarray(inputs["W_top3"]).reshape(M2, P).T),
            put("rows_of_2", np.broadcast_to(np.stack([np.asarray(inputs["b_top2"]).reshape(N2),
                                                       np.asarray(inputs["W_top3"]).reshape(N2)]),
                                             (P, 2, N2)))]
    out = nc.dram_tensor("out_0", (B, 1), mybir.dt.float32, kind="ExternalOutput").ap()
    build(nc, *args, out)
    r = run(nc, [arrays], core_ids=[0])
    return r.results[0]["out_0"]
```
